# Optimizing a Trainium2 kernel written in Bass

```python
import numpy as np
import jax
import jax.numpy as jnp

def _softmax(x, axis=-1):
    return jax.nn.softmax(x, axis=axis)

def _gelu(x):
    return jax.nn.gelu(x, approximate=True)

def _silu(x):
    return jax.nn.silu(x)

def _sigmoid(x):
    return jax.nn.sigmoid(x)

def _layernorm(x, axis=-1, eps=1e-05):
    m = jnp.mean(x, axis=axis, keepdims=True)
    v = jnp.var(x, axis=axis, keepdims=True)
    return (x - m) / jnp.sqrt(v + eps)

def _scatter_add(tgt, idx, src, axis=0):
    return tgt.at[idx].add(src)

def _segment_sum(src, seg, n):
    return jax.ops.segment_sum(src, seg, n)
kernel_name = 'mk_seq_preln_d1_jaxref_r4_4a358e'

def setup_inputs(seed: int=0):
    np.random.seed(seed)
    _w = jnp.asarray

    def _L0_attn_setup():
        import jax, jax.numpy as jnp
        import numpy as np
        from jax import lax
        D = 256
        N = 16
        K = 4
        NH = 16
        NKV = 4
        HD = D // NH
        NREP = NH // NKV
        DFF = 688
        L = 4
        OFF = 0
        EVK = 4
        B = 1
        T = 512
        EPS = 1e-06

        def rmsnorm(x, w):
            return x * lax.rsqrt(jnp.mean(x * x, axis=-1, keepdims=True) + EPS) * w

        def attention(x, wq, wk, wv, wo):
            b, t, _ = x.shape
            q = (x @ wq).reshape(b, t, NH, HD)
            k = jnp.repeat((x @ wk).reshape(b, t, NKV, HD), NREP, axis=2)
            v = jnp.repeat((x @ wv).reshape(b, t, NKV, HD), NREP, axis=2)
            s = jnp.einsum('bqhd,bkhd->bhqk', q, k) * HD ** (-0.5)
            mask = jnp.tril(jnp.ones((t, t), dtype=bool))
            s = jnp.where(mask, s, -jnp.inf)
            w = jax.nn.softmax(s, axis=-1)
            o = jnp.einsum('bhqk,bkhd->bqhd', w, v).reshape(b, t, D)
            return o @ wo

        def ffn(x, wg, wu, wd):
            return jax.nn.silu(x @ wg) * (x @ wu) @ wd

        def dwconv(x, w, bias):
            t = x.shape[1]
            xp = jnp.pad(x, ((0, 0), (K - 1, 0), (0, 0)))
            y = sum((xp[:, k:k + t, :] * w[:, k] for k in range(K)))
            return y + bias

        def ssm(xc, wx, a_log, dskip):
            b, t, _ = xc.shape
            proj = xc @ wx
            delta = jax.nn.softplus(proj[..., :D])
            Bi = proj[..., D:D + N]
            Ci = proj[..., D + N:]
            A = -jnp.exp(a_log)
            a_bar = jnp.exp(delta[..., None] * A)
            b_bar = delta[..., None] * Bi[:, :, None, :]

            def step(h, inp):
                a, bb, xt, ct = inp
                h = a * h + bb * xt[..., None]
                y = jnp.sum(h * ct[:, None, :], axis=-1) + dskip * xt
                return (h, y)
            xs = (jnp.swapaxes(a_bar, 0, 1), jnp.swapaxes(b_bar, 0, 1), jnp.swapaxes(xc, 0, 1), jnp.swapaxes(Ci, 0, 1))
            h0 = jnp.zeros((b, D, N), dtype=xc.dtype)
            h, ys = lax.scan(step, h0, xs)
            return (jnp.swapaxes(ys, 0, 1), h)

        def mamba_block(x, nw, win, cw, cb, wx, a_log, dskip, wout):
            xn = rmsnorm(x, nw)
            xz = xn @ win
            xb, z = (xz[..., :D], xz[..., D:])
            xc = jax.nn.silu(dwconv(xb, cw, cb))
            y, h = ssm(xc, wx, a_log, dskip)
            return (x + y * jax.nn.silu(z) @ wout, h)

        def _reference_tuple_inner(x, attn_norm_w, ffn_norm_w, Wq, Wk, Wv, Wo, Wg, Wu, Wd, m_norm_w, Win, conv_w, conv_b, Wx, A_log, Dp, Wout):
            ai = mi = 0
            hs = []
            for i in range(L):
                if (i - OFF) % EVK == 0:
                    x = x + attention(rmsnorm(x, attn_norm_w[ai]), Wq[ai], Wk[ai], Wv[ai], Wo[ai])
                    x = x + ffn(rmsnorm(x, ffn_norm_w[ai]), Wg[ai], Wu[ai], Wd[ai])
                    ai += 1
                else:
                    x, h = mamba_block(x, m_norm_w[mi], Win[mi], conv_w[mi], conv_b[mi], Wx[mi], A_log[mi], Dp[mi], Wout[mi])
                    hs.append(h)
                    mi += 1
            return (x, jnp.stack(hs))
        key = jax.random.key(seed)
        ks = jax.random.split(key, 16)
        r = lambda k, s: jax.random.normal(k, s, dtype=jnp.float32) * 0.02
        nA, nM = (1, 3)
        a_log = jnp.broadcast_to(jnp.log(jnp.arange(1, N + 1, dtype=jnp.float32)), (D, N))
        return {'x': jax.random.normal(ks[0], (B, T, D), dtype=jnp.float32), 'attn_norm_w': jnp.ones((nA, D), jnp.float32), 'ffn_norm_w': jnp.ones((nA, D), jnp.float32), 'Wq': r(ks[1], (nA, D, D)), 'Wk': r(ks[2], (nA, D, NKV * HD)), 'Wv': r(ks[3], (nA, D, NKV * HD)), 'Wo': r(ks[4], (nA, D, D)), 'Wg': r(ks[5], (nA, D, DFF)), 'Wu': r(ks[6], (nA, D, DFF)), 'Wd': r(ks[7], (nA, DFF, D)), 'm_norm_w': jnp.ones((nM, D), jnp.float32), 'Win': r(ks[8], (nM, D, 2 * D)), 'conv_w': r(ks[9], (nM, D, K)), 'conv_b': jnp.zeros((nM, D), jnp.float32), 'Wx': r(ks[10], (nM, D, D + 2 * N)), 'A_log': jnp.broadcast_to(a_log, (nM, D, N)) + jnp.zeros((nM, D, N), jnp.float32), 'Dp': jnp.ones((nM, D), jnp.float32), 'Wout': r(ks[11], (nM, D, D))}
    _L0_attn_in = _L0_attn_setup()

    def _L0_ffn_setup():
        import jax, jax.numpy as jnp
        import numpy as np
        B, T, D, E, H = (8, 512, 256, 8, 64)
        LN_EPS = 1e-05
        key = jax.random.key(seed)
        ks = jax.random.split(key, 4)
        return {'x': jax.random.normal(ks[0], (B, T, D), dtype=jnp.float32), 'Wg': jax.random.normal(ks[1], (E, D), dtype=jnp.float32) * 0.02, 'ln_scale': jnp.ones((E, D), dtype=jnp.float32), 'ln_bias': jnp.zeros((E, D), dtype=jnp.float32), 'W1': jax.random.normal(ks[2], (E, D, H), dtype=jnp.float32) * 0.02, 'b1': jnp.zeros((E, H), dtype=jnp.float32), 'W2': jax.random.normal(ks[3], (E, H, D), dtype=jnp.float32) * 0.02, 'b2': jnp.zeros((E, D), dtype=jnp.float32)}
    _L0_ffn_in = _L0_ffn_setup()
    _d = {'L0_attn_x': _L0_attn_in['x'], 'L0_attn_attn_norm_w': _L0_attn_in['attn_norm_w'], 'L0_attn_ffn_norm_w': _L0_attn_in['ffn_norm_w'], 'L0_attn_Wq': _L0_attn_in['Wq'], 'L0_attn_Wk': _L0_attn_in['Wk'], 'L0_attn_Wv': _L0_attn_in['Wv'], 'L0_attn_Wo': _L0_attn_in['Wo'], 'L0_attn_Wg': _L0_attn_in['Wg'], 'L0_attn_Wu': _L0_attn_in['Wu'], 'L0_attn_Wd': _L0_attn_in['Wd'], 'L0_attn_m_norm_w': _L0_attn_in['m_norm_w'], 'L0_attn_Win': _L0_attn_in['Win'], 'L0_attn_conv_w': _L0_attn_in['conv_w'], 'L0_attn_conv_b': _L0_attn_in['conv_b'], 'L0_attn_Wx': _L0_attn_in['Wx'], 'L0_attn_A_log': _L0_attn_in['A_log'], 'L0_attn_Dp': _L0_attn_in['Dp'], 'L0_attn_Wout': _L0_attn_in['Wout'], 'L0_ffn_Wg': _L0_ffn_in['Wg'], 'L0_ffn_ln_scale': _L0_ffn_in['ln_scale'], 'L0_ffn_ln_bias': _L0_ffn_in['ln_bias'], 'L0_ffn_W1': _L0_ffn_in['W1'], 'L0_ffn_b1': _L0_ffn_in['b1'], 'L0_ffn_W2': _L0_ffn_in['W2'], 'L0_ffn_b2': _L0_ffn_in['b2']}
    _x0 = _d['L0_attn_x']
    _d['L0_attn_x'] = jax.random.normal(jax.random.fold_in(jax.random.key(seed), 1), (32, 512, 256), dtype=_x0.dtype)
    del _x0
    return _d

def reference(L0_attn_x, L0_attn_attn_norm_w, L0_attn_ffn_norm_w, L0_attn_Wq, L0_attn_Wk, L0_attn_Wv, L0_attn_Wo, L0_attn_Wg, L0_attn_Wu, L0_attn_Wd, L0_attn_m_norm_w, L0_attn_Win, L0_attn_conv_w, L0_attn_conv_b, L0_attn_Wx, L0_attn_A_log, L0_attn_Dp, L0_attn_Wout, L0_ffn_Wg, L0_ffn_ln_scale, L0_ffn_ln_bias, L0_ffn_W1, L0_ffn_b1, L0_ffn_W2, L0_ffn_b2):

    def _L0_attn_ref(x, attn_norm_w, ffn_norm_w, Wq, Wk, Wv, Wo, Wg, Wu, Wd, m_norm_w, Win, conv_w, conv_b, Wx, A_log, Dp, Wout):
        import jax, jax.numpy as jnp
        import numpy as np
        from jax import lax
        D = 256
        N = 16
        K = 4
        NH = 16
        NKV = 4
        HD = D // NH
        NREP = NH // NKV
        DFF = 688
        L = 4
        OFF = 0
        EVK = 4
        B = 1
        T = 512
        EPS = 1e-06

        def rmsnorm(x, w):
            return x * lax.rsqrt(jnp.mean(x * x, axis=-1, keepdims=True) + EPS) * w

        def attention(x, wq, wk, wv, wo):
            b, t, _ = x.shape
            q = (x @ wq).reshape(b, t, NH, HD)
            k = jnp.repeat((x @ wk).reshape(b, t, NKV, HD), NREP, axis=2)
            v = jnp.repeat((x @ wv).reshape(b, t, NKV, HD), NREP, axis=2)
            s = jnp.einsum('bqhd,bkhd->bhqk', q, k) * HD ** (-0.5)
            mask = jnp.tril(jnp.ones((t, t), dtype=bool))
            s = jnp.where(mask, s, -jnp.inf)
            w = jax.nn.softmax(s, axis=-1)
            o = jnp.einsum('bhqk,bkhd->bqhd', w, v).reshape(b, t, D)
            return o @ wo

        def ffn(x, wg, wu, wd):
            return jax.nn.silu(x @ wg) * (x @ wu) @ wd

        def dwconv(x, w, bias):
            t = x.shape[1]
            xp = jnp.pad(x, ((0, 0), (K - 1, 0), (0, 0)))
            y = sum((xp[:, k:k + t, :] * w[:, k] for k in range(K)))
            return y + bias

        def ssm(xc, wx, a_log, dskip):
            b, t, _ = xc.shape
            proj = xc @ wx
            delta = jax.nn.softplus(proj[..., :D])
            Bi = proj[..., D:D + N]
            Ci = proj[..., D + N:]
            A = -jnp.exp(a_log)
            a_bar = jnp.exp(delta[..., None] * A)
            b_bar = delta[..., None] * Bi[:, :, None, :]

            def step(h, inp):
                a, bb, xt, ct = inp
                h = a * h + bb * xt[..., None]
                y = jnp.sum(h * ct[:, None, :], axis=-1) + dskip * xt
                return (h, y)
            xs = (jnp.swapaxes(a_bar, 0, 1), jnp.swapaxes(b_bar, 0, 1), jnp.swapaxes(xc, 0, 1), jnp.swapaxes(Ci, 0, 1))
            h0 = jnp.zeros((b, D, N), dtype=xc.dtype)
            h, ys = lax.scan(step, h0, xs)
            return (jnp.swapaxes(ys, 0, 1), h)

        def mamba_block(x, nw, win, cw, cb, wx, a_log, dskip, wout):
            xn = rmsnorm(x, nw)
            xz = xn @ win
            xb, z = (xz[..., :D], xz[..., D:])
            xc = jax.nn.silu(dwconv(xb, cw, cb))
            y, h = ssm(xc, wx, a_log, dskip)
            return (x + y * jax.nn.silu(z) @ wout, h)

        def _reference_tuple_inner(x, attn_norm_w, ffn_norm_w, Wq, Wk, Wv, Wo, Wg, Wu, Wd, m_norm_w, Win, conv_w, conv_b, Wx, A_log, Dp, Wout):
            ai = mi = 0
            hs = []
            for i in range(L):
                if (i - OFF) % EVK == 0:
                    x = x + attention(rmsnorm(x, attn_norm_w[ai]), Wq[ai], Wk[ai], Wv[ai], Wo[ai])
                    x = x + ffn(rmsnorm(x, ffn_norm_w[ai]), Wg[ai], Wu[ai], Wd[ai])
                    ai += 1
                else:
                    x, h = mamba_block(x, m_norm_w[mi], Win[mi], conv_w[mi], conv_b[mi], Wx[mi], A_log[mi], Dp[mi], Wout[mi])
                    hs.append(h)
                    mi += 1
            return (x, jnp.stack(hs))
        return _reference_tuple_inner(x, attn_norm_w, ffn_norm_w, Wq, Wk, Wv, Wo, Wg, Wu, Wd, m_norm_w, Win, conv_w, conv_b, Wx, A_log, Dp, Wout)[0]

    def _L0_ffn_ref(x, Wg, ln_scale, ln_bias, W1, b1, W2, b2):
        import jax, jax.numpy as jnp
        import numpy as np
        B, T, D, E, H = (8, 512, 256, 8, 64)
        LN_EPS = 1e-05
        Bs, Ts, Ds = x.shape
        xt = x.reshape(Bs * Ts, Ds)
        logits = xt @ Wg.T
        top1 = jnp.argmax(logits, axis=-1)
        mu = jnp.mean(xt, axis=-1, keepdims=True)
        var = jnp.mean(jnp.square(xt - mu), axis=-1, keepdims=True)
        xhat = (xt - mu) * jax.lax.rsqrt(var + LN_EPS)
        n_experts = Wg.shape[0]

        def body(y, p):
            s_e, b_e, w1, bb1, w2, bb2, eid = p
            h = jax.nn.gelu((xhat * s_e + b_e) @ w1 + bb1, approximate=False)
            out = h @ w2 + bb2
            mask = (top1 == eid)[:, None].astype(out.dtype)
            return (y + mask * out, None)
        y0 = jnp.zeros_like(xt)
        y, _ = jax.lax.scan(body, y0, (ln_scale, ln_bias, W1, b1, W2, b2, jnp.arange(n_experts)))
        return y.reshape(Bs, Ts, Ds)
    x = L0_attn_x
    x = x + _L0_attn_ref(_layernorm(x, axis=-1), L0_attn_attn_norm_w, L0_attn_ffn_norm_w, L0_attn_Wq, L0_attn_Wk, L0_attn_Wv, L0_attn_Wo, L0_attn_Wg, L0_attn_Wu, L0_attn_Wd, L0_attn_m_norm_w, L0_attn_Win, L0_attn_conv_w, L0_attn_conv_b, L0_attn_Wx, L0_attn_A_log, L0_attn_Dp, L0_attn_Wout)
    x = x + _L0_ffn_ref(_layernorm(x, axis=-1), L0_ffn_Wg, L0_ffn_ln_scale, L0_ffn_ln_bias, L0_ffn_W1, L0_ffn_b1, L0_ffn_W2, L0_ffn_b2)
    return x

_drawn_inputs = setup_inputs


def setup_inputs(seed=0):
    import zlib

    import numpy as np

    out = dict(_drawn_inputs(seed))
    spreads = {'L0_attn_attn_norm_w': (1.0, 0.6),
     'L0_attn_ffn_norm_w': (1.0, 0.6),
     'L0_attn_m_norm_w': (1.0, 0.6),
     'L0_attn_conv_b': (0.0, 0.8),
     'L0_attn_Dp': (1.0, 0.6),
     'L0_ffn_ln_scale': (1.0, 0.6),
     'L0_ffn_ln_bias': (0.0, 2.0),
     'L0_ffn_b1': (0.0, 2.0),
     'L0_ffn_b2': (0.0, 0.8)}
    factors = {'L0_attn_Wq': 8.0,
     'L0_attn_Wk': 8.0,
     'L0_attn_Wv': 7.808,
     'L0_attn_Wo': 8.0,
     'L0_attn_Wg': 3.375,
     'L0_attn_Wu': 3.336,
     'L0_attn_Wd': 3.342,
     'L0_attn_Win': 8.0,
     'L0_attn_conv_w': 8.0,
     'L0_attn_Wx': 8.0,
     'L0_attn_A_log': 8.0,
     'L0_attn_Wout': 8.0,
     'L0_ffn_W1': 31.608,
     'L0_ffn_W2': 29.736,
     'L0_ffn_Wg': 8.0}
    for name, (base, spread) in spreads.items():
        noise = np.random.default_rng([zlib.crc32(name.encode()), seed]).standard_normal(out[name].shape)
        drawn = base * np.exp(spread * noise) if base else spread * noise
        out[name] = jnp.asarray(drawn.astype(out[name].dtype))
    for name, factor in factors.items():
        out[name] = (out[name] * factor).astype(out[name].dtype)
    return out
```

```python
from contextlib import ExitStack

import concourse.bass as bass
from concourse import mybir

F32 = mybir.dt.float32
BF16 = mybir.dt.bfloat16
ALU = mybir.AluOpType
ACT = mybir.ActivationFunctionType
AX = mybir.AxisListType

P = 128
EPS_RMS = 1e-6
EPS_LN = 1e-5
MASKED = -1e30


def layered_block_kernel(nc, x, attn_norm_w, ffn_norm_w, Wq, Wk, Wv, Wo, Wg, Wu, Wd, m_norm_w, Win, conv_w,
                         conv_b, Wx, A_log, Dp, Wout, gate_W, ln_scale, ln_bias, W1, b1, W2, b2, out):
    B, T, D = x.shape
    HF = D // P
    NC = T // P
    NH, HD = 16, D // 16
    NKV = Wk.shape[2] // HD
    NL = Win.shape[0]
    NS = A_log.shape[2]
    KC = conv_w.shape[2]
    FF = Wg.shape[2]
    FT = -(-FF // P)
    FR = FF - (FT - 1) * P
    NE, _, EH = W1.shape
    ET = NE * EH // P
    G = NS // 2
    SCALE = float(HD) ** -0.5
    TRI = [sum(T - P * j for j in range(k)) for k in range(NC + 1)]

    ctx = ExitStack()
    with ctx:
        def sb(name, shape, dt=F32):
            return ctx.enter_context(nc.sbuf_tensor(name, shape, dt))

        sems = []

        def sem(name):
            s = ctx.enter_context(nc.semaphore(name))
            sems.append(s)
            return s

        win = sb("win", [P, NL, HF, 2 * D])
        wxd = sb("wxd", [P, NL, HF, D + 2 * NS])
        wxbc = sb("wxbc", [P, NL, HF, 3 * 2 * NS])
        wout = sb("wout", [P, NL, HF, D])
        wq = sb("wq", [P, HF, D])
        wk = sb("wk", [P, HF, NKV * HD])
        wkr = sb("wkr", [P, HF, HF, P])
        wv = sb("wv", [P, HF, NKV * HD])
        wo = sb("wo", [P, HF, D])
        wg = sb("wg", [P, HF, FF])
        wu = sb("wu", [P, HF, FF])
        wd = sb("wd", [P, FT, D])
        w1 = sb("w1", [P, HF, NE * EH])
        w2 = sb("w2", [P, ET, D])
        b2r = sb("b2r", [NE, D])
        gwt = sb("gwt", [P, HF, NE])
        anw = sb("anw", [P, HF])
        fnw = sb("fnw", [P, HF])
        mnw = sb("mnw", [P, NL, HF])
        cw = sb("cw", [P, NL, HF, KC])
        cb = sb("cb", [P, NL, HF])
        dp = sb("dp", [P, NL, HF])
        aneg = sb("aneg", [P, NL, HF, NS])
        lns = sb("lns", [P, HF, NE])
        lnb = sb("lnb", [P, HF, NE])
        b1c = sb("b1c", [P, ET])
        ident = sb("ident", [P, P])
        identb = sb("identb", [P, P], BF16)
        mean_w = sb("mean_w", [P, P])
        maskq = sb("maskq", [P, P], BF16)
        maskk = sb("maskk", [P, P], BF16)
        selbc = sb("selbc", [3 * 2 * NS, 2 * NS, P], BF16)
        selh = sb("selh", [P, NH, P], BF16)
        sele = sb("sele", [NE, NE * EH], BF16)
        par = sb("par", [P, 2])
        rank_w = sb("rank_w", [P, NC, NE])
        epsc = sb("epsc", [P, 3])
        res = sb("res", [P, HF, T])
        x0t = sb("x0t", [P, HF, T])
        tA = sb("tA", [P, HF, T])
        tB = sb("tB", [P, HF, T])
        rs = sb("rs", [P, T])
        xbp = sb("xbp", [P, HF, KC - 1 + T])
        delta = xbp[:, :, KC - 1:KC - 1 + T]
        sz = sb("sz", [P, HF, T])
        xc = sb("xc", [P, HF, T])
        bcs = sb("bcs", [3 * 2 * NS, T], BF16)
        bcr = rs[0:4 * NS, :]
        decay = [sb(f"decay{k}", [P, HF, 2, T]) for k in range(2)]
        state = [sb(f"state{k}", [P, HF, 2, T]) for k in range(3)]
        cs = [sb(f"cs{k}", [P, 2, T]) for k in range(2)]
        hid = decay[0]
        lg = sb("lg", [P, NC, NE])
        lmx = sb("lmx", [P, NC, 1])
        oh = sb("oh", [P, NC, NE])
        oht = sz[0:NE, 0, :]
        ohtb = sz[:, 1, :].bitcast(BF16)[0:NE, 0:T]
        x0h = sb("x0h", [P, HF, T])
        hres = sb("hres", [P, HF, T])
        hA = sb("hA", [P, HF, T])
        xio = hA[:].rearrange("p h t -> p (h t)").rearrange("p (c d) -> p c d", c=NC)
        hxn = sb("hxn", [P, HF, T])
        hrs = sb("hrs", [P, T])
        q = sb("q", [P, HF, T])
        kp = sb("kp", [P, 2, HF, T])
        vp = sb("vp", [P, NC, NKV, 2, 64])
        prob = [sb(f"prob{k}", [P, TRI[NC]]) for k in range(2)]
        kpb = prob[0][:, 0:2 * T].bitcast(BF16).rearrange("p (a h t) -> p a h t", a=2, h=HF)
        qb = prob[1][:, 0:T].bitcast(BF16).rearrange("p (h t) -> p h t", h=HF)
        mx = sb("mx", [P, NC, 4, 32])
        negm = sb("negm", [P, T], BF16)
        rinv = hrs[0:32, :]
        of = hA
        gb = kp[:].rearrange("p a h t -> p (a h) t")
        gb2 = q

        def gate_tile(m):
            return gb[:, m, :] if m < 4 else gb2[:, m - 4, :]

        hb = ctx.enter_context(nc.psum_tensor("hb", [P, 3, T], F32))
        bb = ctx.enter_context(nc.psum_tensor("bb", [P, 2, T], F32))
        cbk = ctx.enter_context(nc.psum_tensor("cbk", [P, T], F32))
        yb = ctx.enter_context(nc.psum_tensor("yb", [P, 2, T], F32))

        half = lambda v: v.rearrange("(h p) -> p h", p=P)

        s_load = sem("s_load")
        s_cst = sem("s_cst")
        s_par = sem("s_par")
        s_b1 = sem("s_b1")
        s_ae = sem("s_ae")
        s_dve0 = sem("s_dve0")
        s_pool0 = sem("s_pool0")
        loads = [
            (win[:], Win.rearrange("l (h p) n -> p l h n", p=P)),
            (wxd[:], Wx.rearrange("l (h p) n -> p l h n", p=P)),
            (wout[:], Wout.rearrange("l (h p) n -> p l h n", p=P)),
            (wq[:], Wq[0].rearrange("(h p) n -> p h n", p=P)),
            (wk[:], Wk[0].rearrange("(h p) n -> p h n", p=P)),
            (wv[:], Wv[0].rearrange("(h p) n -> p h n", p=P)),
            (wo[:], Wo[0].rearrange("(h p) n -> p h n", p=P)),
            (wg[:], Wg[0].rearrange("(h p) n -> p h n", p=P)),
            (wu[:], Wu[0].rearrange("(h p) n -> p h n", p=P)),
            (wd[:, 0:FT - 1, :], Wd[0, 0:(FT - 1) * P].rearrange("(m p) n -> p m n", p=P)),
            (wd[0:FR, FT - 1, :], Wd[0, (FT - 1) * P:FF]),
            (w2[:], W2.rearrange("(m a) h n -> (a h) m n", a=P // EH)),
            (b2r[:], b2),
            (anw[:], half(attn_norm_w[0])),
            (fnw[:], half(ffn_norm_w[0])),
            (b1c[:], b1.rearrange("(m a) h -> (a h) m", a=P // EH)),
        ]
        for h in range(HF):
            rows = slice(h * P, h * P + P)
            loads += [
                (w1[:, h, :].rearrange("p (e n) -> p e n", e=NE), W1[:, rows, :].rearrange("e p n -> p e n")),
                (gwt[:, h, :], gate_W[:, rows].rearrange("e p -> p e")),
                (lns[:, h, :], ln_scale[:, rows].rearrange("e p -> p e")),
                (lnb[:, h, :], ln_bias[:, rows].rearrange("e p -> p e")),
                (mnw[:, :, h], m_norm_w[:, rows].rearrange("l p -> p l")),
                (cw[:, :, h, :], conv_w[:, rows, :].rearrange("l p k -> p l k")),
                (cb[:, :, h], conv_b[:, rows].rearrange("l p -> p l")),
                (dp[:, :, h], Dp[:, rows].rearrange("l p -> p l")),
                (aneg[:, :, h, :], A_log[:, rows, :].rearrange("l p n -> p l n")),
            ]

        with nc.Block() as block:
            @block.sync
            def _(sp):
                for dst, src in loads:
                    with nc.allow_non_contiguous_dma(reason="small columns, once"):
                        sp.dma_start(dst, src).then_inc(s_load, 16)

            @block.gpsimd
            def _(pool):
                count = [0]

                def link(ins):
                    count[0] += 1
                    ins.then_inc(s_pool0, 1)
                    pool.wait_ge(s_pool0, count[0])

                def select(t, fill, cond, base, pattern, row):
                    link(pool.affine_select(out=t, in_=t, compare_op=cond, fill=fill, base=base,
                                            pattern=pattern, channel_multiplier=row))

                for t in (ident, identb, maskq, maskk, selbc, selh, sele):
                    link(pool.memset(t[:], 0.0))
                select(ident[:], 1.0, ALU.not_equal, 0, [[-1, P]], 1)
                select(identb[:], 1.0, ALU.not_equal, 0, [[-1, P]], 1)
                select(maskq[:], MASKED, ALU.is_ge, 0, [[-1, P]], 1)
                select(maskk[:], MASKED, ALU.is_ge, 0, [[1, P]], -1)
                for part in range(3):
                    select(selbc[:], 1.0, ALU.not_equal, -2 * NS * part, [[-1, 2 * NS], [0, P]], 1)
                for r in range(4):
                    select(selh[:], 1.0, ALU.not_equal, -32 * r, [[-1, NH], [0, P]], 1)
                select(sele[:].rearrange("e (a n) -> e a n", a=NE), 1.0, ALU.not_equal, 0,
                       [[-1, NE], [0, EH]], 1)
                pool.memset(mean_w[:], 1.0 / D).then_inc(s_cst, 1)

            @block.scalar
            def _(act):
                act.wait_ge(s_load, 16 * len(loads))
                act.activation(aneg[:], aneg[:], ACT.Exp).then_inc(s_ae, 1)

            @block.tensor
            def _(pe):
                pe.wait_ge(s_load, 16 * len(loads))
                for m in range(ET):
                    for h in range(HF):
                        last = pe.matmul(cbk[:, m * NE:(m + 1) * NE], w1[:, h, m * P:(m + 1) * P],
                                         lnb[:, h, :], start=(h == 0), stop=(h == HF - 1))
                last.then_inc(s_b1, 1)

            @block.vector
            def _(dve):
                count = [0]

                def link(ins):
                    count[0] += 1
                    ins.then_inc(s_dve0, 1)
                    dve.wait_ge(s_dve0, count[0])

                for k in range(3):
                    dve.memset(epsc[:, k:k + 1], (EPS_RMS, EPS_LN, 1.0)[k])
                for e in range(NE):
                    dve.memset(rank_w[:, :, e], float(NE - e))
                for k in range(2):
                    dve.memset(decay[k][:, :, :, 0:1], 0.0)
                dve.memset(xbp[:, :, 0:KC - 1], 0.0)
                dve.memset(mx[:], 0.0)
                link(dve.memset(vp[:], 0.0))
                link(dve.memset(vp[:, :, :, 0, 32:32 + HD], 1.0))
                link(dve.memset(vp[:, :, :, 1, 32 + HD:64], 1.0))
                dve.wait_ge(s_cst, 1)
                v = ident[:].rearrange("p (r j) -> p r j", j=2 * HD)
                for e in range(2):
                    dve.tensor_reduce(par[:, e:e + 1], v[:, :, e * HD:(e + 1) * HD], AX.XY, ALU.add)
                dve.wait_ge(s_load, 16 * len(loads))
                for h in range(HF):
                    for w, c in ((wq, anw), (wk, anw), (wv, anw), (wg, fnw), (wu, fnw)):
                        link(dve.tensor_scalar(w[:, h, :], w[:, h, :], c[:, h:h + 1], None, ALU.mult))
                    for l in range(NL):
                        link(dve.tensor_scalar(win[:, l, h, :], win[:, l, h, :], mnw[:, l, h:h + 1], None,
                                               ALU.mult))
                for hf in range(HF):
                    for a in range(2):
                        g = 2 * hf + a
                        for h in range(HF):
                            dve.tensor_copy(
                                wkr[:, h, hf, a * 64:a * 64 + 64].rearrange("p (r j) -> p r j", j=HD),
                                wk[:, h, g * HD:(g + 1) * HD].rearrange("p (r j) -> p r j", r=1)
                                .broadcast_to([P, 4, HD]))
                for k in range(3):
                    dve.tensor_copy(wxbc[:, :, :, k * 2 * NS:(k + 1) * 2 * NS], wxd[:, :, :, D:D + 2 * NS])
                dve.wait_ge(s_ae, 1)
                dve.tensor_scalar(aneg[:], aneg[:], -1.0, None, ALU.mult)
                dve.wait_ge(s_b1, 1)
                for m in range(ET):
                    for a in range(P // EH):
                        rows = slice(a * EH, (a + 1) * EH)
                        e = m * (P // EH) + a
                        dve.tensor_tensor(b1c[rows, m:m + 1], b1c[rows, m:m + 1],
                                          cbk[rows, m * NE + e:m * NE + e + 1], ALU.add)
                for h in range(HF):
                    for e in range(NE):
                        dve.tensor_scalar(w1[:, h, e * EH:(e + 1) * EH], w1[:, h, e * EH:(e + 1) * EH],
                                          lns[:, h, e:e + 1], None, ALU.mult)

        t_own = sem("t_own")
        t_copy = sem("t_copy")
        t_res = sem("t_res")
        t_sq = sem("t_sq")
        t_stat = sem("t_stat")
        t_ln = sem("t_ln")
        t_rs = sem("t_rs")
        t_cen = sem("t_cen")
        t_xn = sem("t_xn")
        t_xb = sem("t_xb")
        t_z = sem("t_z")
        t_xbp = sem("t_xbp")
        t_conv = sem("t_conv")
        t_xc = sem("t_xc")
        t_bc = sem("t_bc")
        t_dl = sem("t_dl")
        t_split = sem("t_split")
        t_abs = sem("t_abs")
        t_delta = sem("t_delta")
        t_u = sem("t_u")
        b_ready = sem("b_ready")
        b_used = sem("b_used")
        c_ready = sem("c_ready")
        c_copied = sem("c_copied")
        decay_ready = sem("decay_ready")
        scanned = sem("scanned")
        weighed = sem("weighed")
        summed = sem("summed")
        t_yg = sem("t_yg")
        t_out = sem("t_out")
        e_lg = sem("e_lg")
        e_oh = sem("e_oh")
        e_oht = sem("e_oht")
        e_ohc = sem("e_ohc")
        e_hp = sem("e_hp")
        e_mask = sem("e_mask")
        e_gelu = sem("e_gelu")
        e_hm = sem("e_hm")
        e_w2 = sem("e_w2")
        e_fin = sem("e_fin")
        e_ft = sem("e_ft")
        e_fc = sem("e_fc")
        e_store = sem("e_store")

        h_x = sem("h_x")
        h_tr = sem("h_tr")
        h_x0 = sem("h_x0")
        h_mean = sem("h_mean")
        h_cen = sem("h_cen")
        h_sq = sem("h_sq")
        h_stat = sem("h_stat")
        h_ln = sem("h_ln")
        h_rs = sem("h_rs")
        h_xn = sem("h_xn")
        h_q = sem("h_q")
        h_qf = sem("h_qf")
        h_k = sem("h_k")
        h_kf = sem("h_kf")
        h_kb = sem("h_kb")
        h_v = sem("h_v")
        h_vp = sem("h_vp")
        h_s = sem("h_s")
        h_mx = sem("h_mx")
        h_mxr = sem("h_mxr")
        h_mt = sem("h_mt")
        h_nm = sem("h_nm")
        h_st = sem("h_st")
        h_p = sem("h_p")
        h_pv = sem("h_pv")
        h_dl = sem("h_dl")
        h_ri = sem("h_ri")
        h_on = sem("h_on")
        h_wo = sem("h_wo")
        h_r2 = sem("h_r2")
        h_g = sem("h_g")
        h_gc = sem("h_gc")
        h_si = sem("h_si")
        h_u = sem("h_u")
        h_h = sem("h_h")
        h_wd = sem("h_wd")

        MAXB = [[(0, 0), (P, 2)], [(0, 3)], [(0, 1)]]
        EXPB = [[(0, 0)], [(0, 1), (T - P, 3)], [(0, 2)]]
        NB = 3

        def turn(head, tail):
            do_h, do_t = head is not None, tail is not None

            def sp_program(sp):
                if do_h:
                    sp.dma_start(xio, x[bass.ds(head, 1)].rearrange("b (c p) d -> p (b c) d", p=P)
                                 ).then_inc(h_x, 16)
                if do_t:
                    sp.wait_ge(e_fc, 2)
                    sp.dma_start(out[bass.ds(tail, 1)].rearrange("b (c p) d -> p (b c) d", p=P),
                                 state[0][:].rearrange("p h n t -> p (h n t)")[:, 0:NC * D]
                                 .rearrange("p (c d) -> p c d", c=NC)).then_inc(e_store, 16)
                    sp.wait_ge(e_store, 16)

            def pe_program(pe):
                def project(dst, w, src, cols, n=P, stop=True):
                    for h in range(HF):
                        last = pe.matmul(dst, w[:, h, cols:cols + n], src[:, h, :], start=(h == 0),
                                         stop=(h == HF - 1))
                    return last

                def stat(dst, src):
                    for h in range(HF):
                        last = pe.matmul(dst, mean_w[:], src[:, h, :], start=(h == 0), stop=(h == HF - 1))
                    return last

                def pre(l):
                    wl, xl = win[:, l], wxd[:, l]
                    pe.wait_ge(t_sq, l + 1)
                    stat(yb[:, 0, :], tA).then_inc(t_stat, 1)
                    pe.wait_ge(t_xn, l + 1)
                    for j in range(2):
                        last = project(bb[:, j, :], wl, tB, j * P)
                    last.then_inc(t_xb, 1)
                    project(cbk[:], wl, tB, 2 * P)
                    project(yb[:, 1, :], wl, tB, 3 * P).then_inc(t_z, 1)

                def pre_x(l):
                    pe.wait_ge(t_xc, l + 1)
                    project(cbk[0:3 * 2 * NS, :], wxbc[:, l], xc, 0, 3 * 2 * NS).then_inc(t_bc, 1)
                    for j in range(2):
                        last = project(bb[:, j, :], wxd[:, l], xc, j * P)
                    last.then_inc(t_dl, 1)

                def spread(l, g):
                    k = G * l + g
                    if g == 0:
                        pe.wait_ge(t_split, l + 1)
                        pe.wait_ge(t_delta, l + 1)
                    for j in range(2):
                        n = 2 * g + j
                        if g > 0:
                            pe.wait_ge(b_used, 2 * (k - 1) + j + 1)
                        pe.matmul(bb[:, j, :], selbc[:, n, :], bcs[:], start=True, stop=True
                                  ).then_inc(b_ready, 1)
                        if n > 0:
                            pe.wait_ge(c_copied, 2 * k + j)
                        pe.matmul(cbk[:], selbc[:, NS + n, :], bcs[:], start=True, stop=True
                                  ).then_inc(c_ready, 1)

                def sum_states(l, g):
                    k = G * l + g
                    for h in range(HF):
                        pe.wait_ge(weighed, 2 * k + h + 1)
                        for j in range(2):
                            last = pe.matmul(yb[:, h, :], ident[:], state[k % 3][:, h, j, :],
                                             start=(g == 0 and j == 0), stop=(g == G - 1 and j == 1))
                    last.then_inc(summed, 1)

                def post(l):
                    pe.wait_ge(t_yg, l + 1)
                    for j in range(2):
                        last = project(bb[:, j, :], wout[:, l], tA, j * P)
                    last.then_inc(t_out, 1)

                def experts_norm():
                    pe.wait_ge(t_res, NL + 2)
                    stat(yb[:, 0, :], x0t).then_inc(t_stat, 1)
                    pe.wait_ge(t_sq, NL + 1)
                    stat(yb[:, 1, :], tA).then_inc(t_stat, 1)
                    pe.wait_ge(t_xn, NL + 1)
                    for c in range(NC):
                        for h in range(HF):
                            last = pe.matmul(cbk[:, c * NE:(c + 1) * NE], tB[:, h, c * P:(c + 1) * P],
                                             gwt[:, h, :], start=(h == 0), stop=(h == HF - 1))
                    last.then_inc(e_lg, 1)
                    pe.wait_ge(t_sq, NL + 2)
                    stat(yb[:, 0, :], tA).then_inc(t_stat, 1)

                def experts():
                    pe.wait_ge(e_oh, 1)
                    for c in range(NC):
                        last = pe.transpose(cbk[0:NE, c * P:(c + 1) * P], oh[:, c, :], ident[:])
                    last.then_inc(e_oht, 1)
                    pe.wait_ge(t_xn, NL + 2)
                    for m in range(ET):
                        if m >= 2:
                            pe.wait_ge(e_gelu, m - 1)
                        project(bb[:, m % 2, :], w1, tB, m * P).then_inc(e_hp, 1)
                        if m == 0:
                            pe.wait_ge(e_ohc, 1)
                        if m >= 2:
                            pe.wait_ge(e_hm, m - 1)
                        pe.matmul(yb[:, m % 2, :], sele[:, m * P:(m + 1) * P], ohtb, start=True,
                                  stop=True).then_inc(e_mask, 1)
                    pe.wait_ge(e_hm, ET)
                    for j in range(2):
                        for m in range(ET):
                            pe.matmul(bb[:, j, :], w2[:, m, j * P:(j + 1) * P],
                                      hid[:, m // 2, m % 2, :], start=(m == 0), stop=False)
                        last = pe.matmul(bb[:, j, :], b2r[:, j * P:(j + 1) * P], oht, start=False, stop=True)
                    last.then_inc(e_w2, 1)
                    pe.wait_ge(e_fin, 1)
                    for b in range(2):
                        for c in range(2):
                            for h in range(HF):
                                last = pe.transpose(yb[:, b, c * D + h * P:c * D + h * P + P],
                                                    tA[:, h, (2 * b + c) * P:(2 * b + c + 1) * P], ident[:])
                        last.then_inc(e_ft, 1)

                def h_load():
                    pe.wait_ge(h_x, 16)
                    for h in range(HF):
                        for c in range(NC):
                            last = pe.transpose(hb[:, h, c * P:(c + 1) * P], xio[:, c, h * P:(h + 1) * P],
                                                ident[:])
                    last.then_inc(h_tr, 1)
                    pe.wait_ge(h_x0, 1)
                    stat(hb[:, 2, :], x0h).then_inc(h_mean, 1)

                def h_norm(m, bank):
                    pe.wait_ge(h_sq, m + 1)
                    stat(hb[:, bank, :], hxn).then_inc(h_stat, 1)

                def h_qkv():
                    pe.wait_ge(h_xn, 1)
                    for j in range(2):
                        last = project(hb[:, j, :], wq, hxn, j * P)
                    last.then_inc(h_q, 1)
                    for j in range(2):
                        if j == 1:
                            pe.wait_ge(h_qf, 1)
                        for h in range(HF):
                            last = pe.matmul(hb[:, 2 if j == 0 else 0, :], wkr[:, h, j, :], hxn[:, h, :],
                                             start=(h == 0), stop=(h == HF - 1))
                        last.then_inc(h_k, 1)
                    for c in range(NC):
                        for h in range(HF):
                            last = pe.matmul(hb[:, 1, c * 64:(c + 1) * 64], hxn[:, h, c * P:(c + 1) * P],
                                             wv[:, h, :], start=(h == 0), stop=(h == HF - 1))
                    last.then_inc(h_v, 1)

                def h_max(h):
                    r, par_, hf = 32 * ((h % 8) // 2), h % 2, h // 8
                    if h == 0:
                        pe.wait_ge(h_kf, 2)
                        pe.wait_ge(h_kb, 1)
                        pe.wait_ge(h_vp, 1)
                    for b in range(NB):
                        if h > 0:
                            pe.wait_ge(h_mx, NB * (h - 1) + b + 1)
                        for col, c in MAXB[b]:
                            n = (c + 1) * P
                            pe.matmul(hb[:, b, col:col + n], qb[r:r + 32, hf, c * P:n],
                                      kpb[r:r + 32, par_, hf, 0:n], start=True, stop=False)
                            last = pe.matmul(hb[:, b, col + n - P:col + n], identb[:], maskq[:],
                                             start=False, stop=True)
                        last.then_inc(h_s, 1)

                def h_maxrow():
                    pe.wait_ge(h_mxr, 1)
                    for c in range(NC):
                        last = pe.transpose(hb[:, 0, c * P:(c + 1) * P],
                                            mx[:, c, :, :].rearrange("p r h -> p (r h)"), ident[:])
                    last.then_inc(h_mt, 1)

                def h_scores(h):
                    r, par_, hf = 32 * ((h % 8) // 2), h % 2, h // 8
                    if h == 0:
                        pe.wait_ge(h_nm, 1)
                    for b in range(NB):
                        w = NB * h + b
                        if w >= 2:
                            pe.wait_ge(h_p, w - 1)
                        for col, c in EXPB[b]:
                            n = T - c * P
                            dst = hb[:, w % 2, col:col + n]
                            pe.matmul(dst, kp[r:r + 32, par_, hf, c * P:(c + 1) * P], q[r:r + 32, hf, c * P:T],
                                      start=True, stop=False)
                            pe.matmul(dst, selh[r:r + 32, h, :], negm[r:r + 32, c * P:T], start=False, stop=False)
                            last = pe.matmul(hb[:, w % 2, col:col + P], identb[:], maskk[:], start=False,
                                             stop=True)
                        last.then_inc(h_st, 1)

                def h_values(h):
                    pe.wait_ge(h_p, NB * (h + 1))
                    if h % 2 == 0 and h > 0:
                        pe.wait_ge(h_on, h // 2)
                    for c in range(NC):
                        last = pe.matmul(hb[0:64, 2, c * P:T], vp[:, c, h // 4, h % 2, :],
                                         prob[h % 2][:, TRI[c]:TRI[c + 1]],
                                         start=(c == 0 and h % 2 == 0), stop=(c == NC - 1 and h % 2 == 1))
                    last.then_inc(h_pv, 1)

                def h_attn_out():
                    pe.wait_ge(h_on, NH // 2)
                    for j in range(2):
                        last = project(hb[:, j, :], wo, of, j * P)
                    last.then_inc(h_wo, 1)

                def h_ffn_gate():
                    h_norm(2, 2)
                    pe.wait_ge(h_xn, 2)
                    for m in range(FT):
                        n = P if m < FT - 1 else FR
                        if m == 2:
                            pe.wait_ge(h_rs, 3)
                        if m >= 3:
                            pe.wait_ge(h_gc, m - 2)
                        project(hb[0:n, m % 3, :], wg, hxn, m * P, n).then_inc(h_g, 1)

                def h_ffn_up():
                    for m in range(FT):
                        n = P if m < FT - 1 else FR
                        pe.wait_ge(h_gc, m + 4 if m < 3 else FT)
                        if m >= 3:
                            pe.wait_ge(h_h, m - 2)
                        project(hb[0:n, m % 3, :], wu, hxn, m * P, n).then_inc(h_u, 1)

                def h_ffn_down():
                    pe.wait_ge(h_h, FT)
                    for j in range(2):
                        for m in range(FT):
                            n = P if m < FT - 1 else FR
                            last = pe.matmul(hb[:, j, :], wd[0:n, m, j * P:(j + 1) * P], gate_tile(m)[0:n],
                                             start=(m == 0), stop=(m == FT - 1))
                    last.then_inc(h_wd, 1)

                def head_step(n):
                    if not do_h:
                        return
                    if n == 0:
                        h_load()
                        h_norm(0, 0)
                        h_norm(1, 1)
                        h_qkv()
                    elif n <= 8:
                        h_max(2 * n - 2)
                        h_max(2 * n - 1)
                    elif n == 9:
                        h_maxrow()
                        h_scores(0)
                    elif n <= 24:
                        h_scores(n - 9)
                        h_values(n - 10)
                    elif n == 25:
                        h_values(NH - 1)
                        h_attn_out()
                    elif n == 26:
                        h_ffn_gate()
                        h_ffn_up()
                        h_ffn_down()

                if do_t:
                    for l in range(NL):
                        pre(l)
                        head_step(9 * l)
                        pre_x(l)
                        spread(l, 0)
                        for g in range(G):
                            if g < G - 1:
                                spread(l, g + 1)
                            head_step(9 * l + 1 + g)
                            if g > 0:
                                sum_states(l, g - 1)
                        sum_states(l, G - 1)
                        post(l)
                    experts_norm()
                    experts()
                else:
                    for n in range(27):
                        head_step(n)

            def act_program(act):
                def root(dst, src, eps, ln, rs_sem, n):
                    act.activation(dst, src, ACT.Ln, bias=epsc[:, eps:eps + 1]).then_inc(ln, 1)
                    act.wait_ge(ln, n)
                    act.activation(dst, dst, ACT.Exp, scale=-0.5).then_inc(rs_sem, 1)

                def pre(l):
                    act.wait_ge(t_res, l + 1)
                    act.activation(tA[:], res[:], ACT.Square).then_inc(t_sq, 1)
                    act.wait_ge(t_stat, l + 1)
                    root(rs[:], yb[:, 0, :], 0, t_ln, t_rs, l + 1)
                    act.wait_ge(t_xb, l + 1)
                    act.activation(xbp[:, :, KC - 1:KC - 1 + T], bb[:], ACT.Copy).then_inc(t_xbp, 1)
                    act.wait_ge(t_z, l + 1)
                    act.activation(sz[:, 0, :], cbk[:], ACT.Silu)
                    act.activation(sz[:, 1, :], yb[:, 1, :], ACT.Silu)
                    act.wait_ge(t_conv, l + 1)
                    act.activation(xc[:], tA[:], ACT.Silu).then_inc(t_xc, 1)

                def softplus(l):
                    act.wait_ge(t_dl, l + 1)
                    act.activation(tA[:], bb[:], ACT.Abs).then_inc(t_abs, 1)
                    act.wait_ge(t_abs, 3 * l + 1)
                    act.activation(tA[:], tA[:], ACT.Exp, scale=-1.0).then_inc(t_abs, 1)
                    act.wait_ge(t_abs, 3 * l + 2)
                    act.activation(tA[:], tA[:], ACT.Ln, bias=epsc[:, 2:3]).then_inc(t_abs, 1)

                def step(l, g):
                    k = G * l + g
                    if g == 0:
                        act.wait_ge(t_delta, l + 1)
                    for j in range(2):
                        if k >= 2:
                            act.wait_ge(weighed, 2 * (k - 1))
                        act.wait_ge(c_ready, 2 * k + j + 1)
                        act.activation(cs[k % 2][:, j, :], cbk[:], ACT.Copy).then_inc(c_copied, 1)
                    if k >= 2:
                        act.wait_ge(scanned, k - 1)
                    for h in range(HF):
                        for j in range(2):
                            last = act.activation(decay[k % 2][:, h, j, 1:T], delta[:, h, 1:T], ACT.Exp,
                                                  scale=aneg[:, l, h, 2 * g + j:2 * g + j + 1])
                    last.then_inc(decay_ready, 1)

                def experts_norm():
                    act.wait_ge(t_cen, 1)
                    act.activation(tA[:], tB[:], ACT.Square).then_inc(t_sq, 1)
                    act.wait_ge(t_stat, NL + 2)
                    root(rs[:], yb[:, 1, :], 1, t_ln, t_rs, NL + 1)
                    act.wait_ge(t_xn, NL + 1)
                    act.activation(tA[:], tB[:], ACT.Square).then_inc(t_sq, 1)
                    act.wait_ge(t_stat, NL + 3)
                    root(rs[:], yb[:, 0, :], 1, t_ln, t_rs, NL + 2)

                def experts():
                    act.wait_ge(e_oht, 1)
                    act.activation(oht, cbk[0:NE, :], ACT.Copy)
                    act.activation(ohtb, cbk[0:NE, :], ACT.Copy).then_inc(e_ohc, 1)
                    for m in range(ET):
                        act.wait_ge(e_hp, m + 1)
                        act.activation(hid[:, m // 2, m % 2, :], bb[:, m % 2, :], ACT.Gelu,
                                       bias=b1c[:, m:m + 1]).then_inc(e_gelu, 1)
                    fin = state[0][:].rearrange("p h n t -> p (h n t)")
                    for b in range(2):
                        act.wait_ge(e_ft, b + 1)
                        act.activation(fin[:, b * 2 * D:(b + 1) * 2 * D], yb[:, b, :], ACT.Copy
                                       ).then_inc(e_fc, 1)

                def h_load():
                    act.wait_ge(h_tr, 1)
                    if do_t:
                        act.wait_ge(t_copy, 2)
                    act.activation(x0h[:], hb[:, 0:2, :], ACT.Copy).then_inc(h_x0, 1)

                def h_norm(m, src, bank, eps):
                    act.activation(hxn[:], src, ACT.Square).then_inc(h_sq, 1)
                    act.wait_ge(h_stat, m + 1)
                    root(hrs[:], hb[:, bank, :], eps, h_ln, h_rs, m + 1)

                def h_qkv():
                    act.wait_ge(h_q, 1)
                    act.activation(q[:], hb[:, 0:2, :], ACT.Copy).then_inc(h_qf, 1)
                    for j in range(2):
                        act.wait_ge(h_k, j + 1)
                        for e in range(2):
                            last = act.activation(kp[:, e, j, :], hb[:, 2 if j == 0 else 0, :], ACT.Copy,
                                                  scale=par[:, e:e + 1])
                        last.then_inc(h_kf, 1)

                def h_negmax():
                    act.wait_ge(h_mt, 1)
                    act.activation(negm[:], hb[:, 0, :], ACT.Copy, scale=-1.0).then_inc(h_nm, 1)

                def h_probs(h):
                    if h >= 2:
                        act.wait_ge(h_pv, h - 1)
                    for b in range(NB):
                        w = NB * h + b
                        act.wait_ge(h_st, w + 1)
                        for col, c in EXPB[b]:
                            last = act.activation(prob[h % 2][:, TRI[c]:TRI[c + 1]],
                                                  hb[:, w % 2, col:col + T - c * P], ACT.Exp, scale=SCALE)
                        last.then_inc(h_p, 1)

                def h_inv(p):
                    act.wait_ge(h_pv, 2 * p + 2)
                    if p > 0:
                        act.wait_ge(h_on, p)
                    act.activation(rinv, hb[32:64, 2, :], ACT.Ln).then_inc(h_dl, 1)
                    act.wait_ge(h_dl, p + 1)
                    act.activation(rinv, rinv, ACT.Exp, scale=-1.0).then_inc(h_ri, 1)

                def h_ffn():
                    act.wait_ge(h_r2, 1)
                    h_norm(2, hres[:], 2, 0)
                    for m in range(FT):
                        n = P if m < FT - 1 else FR
                        act.wait_ge(h_g, m + 1)
                        act.activation(gate_tile(m)[0:n], hb[0:n, m % 3, :], ACT.Copy).then_inc(h_gc, 1)
                    act.wait_ge(h_gc, FT)
                    act.activation(gb, gb, ACT.Silu)
                    act.activation(gb2[:, 0, :], gb2[:, 0, :], ACT.Silu)
                    act.activation(gb2[0:FR, 1, :], gb2[0:FR, 1, :], ACT.Silu).then_inc(h_si, 1)

                def head_step(n):
                    if not do_h:
                        return
                    if n == 0:
                        h_load()
                        act.wait_ge(h_cen, 1)
                        h_norm(0, hA[:], 0, 1)
                        act.wait_ge(h_cen, 2)
                        h_norm(1, hres[:], 1, 0)
                        h_qkv()
                    elif n == 9:
                        h_negmax()
                        h_probs(0)
                    elif 10 <= n <= 24:
                        h_probs(n - 9)
                        if n % 2 == 1:
                            h_inv((n - 11) // 2)
                    elif n == 25:
                        h_inv(NH // 2 - 1)
                    elif n == 26:
                        h_ffn()

                if do_t:
                    for l in range(NL):
                        pre(l)
                        head_step(9 * l)
                        softplus(l)
                        step(l, 0)
                        for g in range(G):
                            if g < G - 1:
                                step(l, g + 1)
                            head_step(9 * l + 1 + g)
                    experts_norm()
                    experts()
                else:
                    for n in range(27):
                        head_step(n)

            def dve_program(dve):
                own = [0]

                def link(ins):
                    own[0] += 1
                    ins.then_inc(t_own, 1)
                    dve.wait_ge(t_own, own[0])

                def over_halves(v, n=HF):
                    return v.rearrange("p (a t) -> p a t", a=1).broadcast_to([P, n, T])

                def take():
                    dve.tensor_copy(res[:], hres[:]).then_inc(t_res, 1)
                    dve.tensor_copy(x0t[:], x0h[:]).then_inc(t_copy, 2)

                def pre(l):
                    dve.wait_ge(t_rs, l + 1)
                    dve.tensor_tensor(tB[:], res[:], over_halves(rs[:]), ALU.mult).then_inc(t_xn, 1)

                def conv(l):
                    dve.wait_ge(t_xbp, l + 1)
                    for h in range(HF):
                        last = dve.tensor_scalar(tA[:, h, :], xbp[:, h, 0:T], cw[:, l, h, 0:1],
                                                 cb[:, l, h:h + 1], ALU.mult, ALU.add)
                    for k in range(1, KC):
                        link(last)
                        for h in range(HF):
                            last = dve.scalar_tensor_tensor(out=tA[:, h, :], in0=xbp[:, h, k:k + T],
                                                            scalar=cw[:, l, h, k:k + 1], in1=tA[:, h, :],
                                                            op0=ALU.mult, op1=ALU.add)
                    last.then_inc(t_conv, 1)

                def split(l):
                    dve.wait_ge(t_bc, l + 1)
                    link(dve.tensor_copy(bcs[:], cbk[0:6 * NS, :]))
                    link(dve.tensor_tensor(bcr, cbk[0:4 * NS, :], bcs[0:4 * NS, :], ALU.subtract))
                    link(dve.tensor_copy(bcs[0:4 * NS, :], bcr))
                    dve.tensor_tensor(bcs[0:2 * NS, :], bcr[0:2 * NS, :], bcs[0:2 * NS, :],
                                      ALU.subtract).then_inc(t_split, 1)
                    dve.wait_ge(t_abs, 3 * l + 3)
                    dve.scalar_tensor_tensor(out=delta, in0=bb[:], scalar=0.0, in1=tA[:], op0=ALU.max,
                                             op1=ALU.add).then_inc(t_delta, 1)
                    dve.wait_ge(t_delta, l + 1)
                    dve.tensor_tensor(tB[:], delta, xc[:], ALU.mult).then_inc(t_u, 1)
                    dve.wait_ge(t_u, l + 1)

                def step(l, g):
                    k = G * l + g
                    if k >= 3:
                        dve.wait_ge(summed, k - 2)
                    for j in range(2):
                        dve.wait_ge(b_ready, 2 * k + j + 1)
                        dve.tensor_tensor(state[k % 3][:, :, j, :], tB[:], over_halves(bb[:, j, :]),
                                          ALU.mult).then_inc(b_used, 1)
                    dve.wait_ge(b_used, 2 * k + 2)
                    dve.wait_ge(decay_ready, k + 1)
                    flat = state[k % 3][:].rearrange("p h n t -> p (h n t)")
                    dve.tensor_tensor_scan(flat, decay[k % 2][:].rearrange("p h n t -> p (h n t)"), flat, 0.0,
                                           ALU.mult, ALU.add).then_inc(scanned, 1)

                def post(l):
                    dve.wait_ge(summed, G * (l + 1))
                    for h in range(HF):
                        last = dve.scalar_tensor_tensor(out=tA[:, h, :], in0=xc[:, h, :],
                                                        scalar=dp[:, l, h:h + 1], in1=yb[:, h, :],
                                                        op0=ALU.mult, op1=ALU.add)
                    link(last)
                    dve.tensor_tensor(tA[:], tA[:], sz[:], ALU.mult).then_inc(t_yg, 1)
                    dve.wait_ge(t_out, l + 1)
                    dve.tensor_tensor(res[:], res[:], bb[:], ALU.add).then_inc(t_res, 1)

                def experts_norm():
                    dve.wait_ge(t_res, NL + 1)
                    dve.tensor_tensor(x0t[:], x0t[:], res[:], ALU.add).then_inc(t_res, 1)
                    dve.wait_ge(t_stat, NL + 1)
                    dve.wait_ge(t_res, NL + 2)
                    dve.tensor_tensor(tB[:], x0t[:], over_halves(yb[:, 0, :]), ALU.subtract
                                      ).then_inc(t_cen, 1)
                    dve.wait_ge(t_cen, 1)
                    dve.wait_ge(t_rs, NL + 1)
                    dve.tensor_tensor(tB[:], tB[:], over_halves(rs[:]), ALU.mult).then_inc(t_xn, 1)

                def experts_pick():
                    dve.wait_ge(e_lg, 1)
                    link(dve.tensor_copy(lg[:], cbk[:, 0:NC * NE].rearrange("p (c e) -> p c e", c=NC)))
                    link(dve.tensor_reduce(lmx[:], lg[:], AX.X, ALU.max))
                    link(dve.tensor_tensor(lg[:], lg[:], lmx[:].broadcast_to([P, NC, NE]), ALU.is_ge))
                    link(dve.tensor_tensor(lg[:], lg[:], rank_w[:], ALU.mult))
                    link(dve.tensor_reduce(lmx[:], lg[:], AX.X, ALU.max))
                    dve.tensor_tensor(oh[:], lg[:], lmx[:].broadcast_to([P, NC, NE]), ALU.is_equal
                                      ).then_inc(e_oh, 1)

                def experts():
                    dve.wait_ge(t_rs, NL + 2)
                    dve.tensor_tensor(tB[:], tB[:], over_halves(rs[:]), ALU.mult).then_inc(t_xn, 1)
                    for m in range(ET):
                        dve.wait_ge(e_gelu, m + 1)
                        dve.wait_ge(e_mask, m + 1)
                        v = hid[:, m // 2, m % 2, :]
                        dve.tensor_tensor(v, v, yb[:, m % 2, :], ALU.mult).then_inc(e_hm, 1)
                    dve.wait_ge(e_w2, 1)
                    dve.tensor_tensor(tA[:], x0t[:], bb[:], ALU.add).then_inc(e_fin, 1)
                    for k in range(1):
                        dve.memset(hid[:, :, :, 0:1], 0.0).then_inc(t_copy, 1)

                def h_load():
                    dve.wait_ge(h_mean, 1)
                    dve.tensor_tensor(hA[:], x0h[:], over_halves(hb[:, 2, :]), ALU.subtract).then_inc(h_cen, 1)
                    dve.wait_ge(h_cen, 1)
                    dve.wait_ge(h_rs, 1)
                    dve.tensor_tensor(hres[:], hA[:], over_halves(hrs[:]), ALU.mult).then_inc(h_cen, 1)
                    dve.wait_ge(h_cen, 2)
                    dve.wait_ge(h_rs, 2)
                    dve.tensor_tensor(hxn[:], hres[:], over_halves(hrs[:]), ALU.mult).then_inc(h_xn, 1)

                def h_qkv():
                    dve.wait_ge(h_qf, 1)
                    dve.tensor_copy(qb, q[:])
                    dve.wait_ge(h_kf, 2)
                    dve.tensor_copy(kpb, kp[:]).then_inc(h_kb, 1)
                    dve.wait_ge(h_v, 1)
                    for e in range(2):
                        last = dve.tensor_copy(
                            vp[:, :, :, e, e * HD:(e + 1) * HD],
                            hb[:, 1, 0:NC * 64].rearrange("p (c g j) -> p c g j", c=NC, g=NKV))
                    last.then_inc(h_vp, 1)

                def h_max(h):
                    for b in range(NB):
                        dve.wait_ge(h_s, NB * h + b + 1)
                        for col, c in MAXB[b]:
                            last = dve.tensor_reduce(mx[:, c, 0, h:h + 1], hb[:, b, col:col + (c + 1) * P], AX.X,
                                                     ALU.max)
                        last.then_inc(h_mx, 1)
                    if h == NH - 1:
                        dve.wait_ge(h_mx, NB * NH)
                        for r in range(1, 4):
                            last = dve.tensor_copy(mx[:, :, r, 0:NH], mx[:, :, 0, 0:NH])
                        last.then_inc(h_mxr, 1)

                def h_normalise(p):
                    dve.wait_ge(h_ri, p + 1)
                    r = 32 * (p % 4)
                    dve.tensor_tensor(of[r:r + 32, p // 4, :], hb[0:32, 2, :], rinv, ALU.mult
                                      ).then_inc(h_on, 1)

                def h_attn_out():
                    dve.wait_ge(h_wo, 1)
                    dve.tensor_tensor(hres[:], hres[:], hb[:, 0:2, :], ALU.add).then_inc(h_r2, 1)

                def h_ffn():
                    dve.wait_ge(h_rs, 3)
                    dve.wait_ge(h_r2, 1)
                    dve.tensor_tensor(hxn[:], hres[:], over_halves(hrs[:]), ALU.mult).then_inc(h_xn, 1)
                    dve.wait_ge(h_si, 1)
                    for m in range(FT):
                        n = P if m < FT - 1 else FR
                        dve.wait_ge(h_u, m + 1)
                        v = gate_tile(m)[0:n]
                        dve.tensor_tensor(v, v, hb[0:n, m % 3, :], ALU.mult).then_inc(h_h, 1)
                    dve.wait_ge(h_wd, 1)
                    dve.tensor_tensor(hres[:], hres[:], hb[:, 0:2, :], ALU.add).then_inc(h_r2, 1)

                def head_step(n):
                    if not do_h:
                        return
                    if n == 0:
                        h_load()
                        h_qkv()
                    elif n <= 8:
                        h_max(2 * n - 2)
                        h_max(2 * n - 1)
                    elif 11 <= n <= 23 and n % 2 == 1:
                        h_normalise((n - 11) // 2)
                    elif n == 25:
                        h_normalise(NH // 2 - 1)
                        h_attn_out()
                    elif n == 26:
                        h_ffn()

                if do_t:
                    take()
                    for l in range(NL):
                        pre(l)
                        conv(l)
                        head_step(9 * l)
                        split(l)
                        for g in range(G):
                            step(l, g)
                            head_step(9 * l + 1 + g)
                        post(l)
                    experts_norm()
                    experts_pick()
                    experts()
                else:
                    for n in range(27):
                        head_step(n)

            def pool_program(pool):
                for l in range(NL):
                    for g in range(G):
                        k = G * l + g
                        pool.wait_ge(scanned, k + 1)
                        pool.wait_ge(c_copied, 2 * k + 2)
                        for h in range(HF):
                            v = state[k % 3][:, h, :, :]
                            pool.tensor_tensor(v, v, cs[k % 2][:], ALU.mult).then_inc(weighed, 1)

            with nc.Block() as block:
                block.sync(sp_program)
                block.tensor(pe_program)
                block.scalar(act_program)
                block.vector(dve_program)
                if do_t:
                    block.gpsimd(pool_program)

        turn_sems = sems[7:]

        def clear():
            for s in turn_sems:
                nc.sync.sem_clear(s)
            nc.all_engine_barrier()

        turn(0, None)
        clear()
        if B > 1:
            with nc.Fori(0, B - 1) as i:
                turn(i + 1, i)
                clear()
        turn(None, B - 1)


_INS = ["L0_attn_x", "L0_attn_attn_norm_w", "L0_attn_ffn_norm_w", "L0_attn_Wq", "L0_attn_Wk", "L0_attn_Wv",
        "L0_attn_Wo", "L0_attn_Wg", "L0_attn_Wu", "L0_attn_Wd", "L0_attn_m_norm_w", "L0_attn_Win",
        "L0_attn_conv_w", "L0_attn_conv_b", "L0_attn_Wx", "L0_attn_A_log", "L0_attn_Dp", "L0_attn_Wout",
        "L0_ffn_Wg", "L0_ffn_ln_scale", "L0_ffn_ln_bias", "L0_ffn_W1", "L0_ffn_b1", "L0_ffn_W2", "L0_ffn_b2"]


def kernel(**inputs):
    import numpy as _np
    import concourse.bacc as _bacc
    from concourse import mybir as _mybir
    from concourse.bass_utils import run_bass_kernel_spmd as _run

    nc = _bacc.Bacc("TRN2", target_bir_lowering=False, num_devices=1)
    arrays, args = {}, []
    for name in _INS:
        a = _np.ascontiguousarray(inputs[name])
        arrays[f"in_{name}_dram"] = a
        args.append(nc.dram_tensor(f"in_{name}_dram", a.shape, _mybir.dt.from_np(a.dtype), kind="ExternalInput").ap())
    shape = inputs["L0_attn_x"].shape
    args.append(nc.dram_tensor("out_0_dram", shape, _mybir.dt.float32, kind="ExternalOutput").ap())
    layered_block_kernel(nc, *args)
    r = _run(nc, [arrays], core_ids=[0])
    return r.results[0]["out_0_dram"]
```

```python
from contextlib import ExitStack

import concourse.bass as bass
from concourse import mybir

F32 = mybir.dt.float32
BF16 = mybir.dt.bfloat16
ALU = mybir.AluOpType
ACT = mybir.ActivationFunctionType
AX = mybir.AxisListType

P = 128
EPS_RMS = 1e-6
EPS_LN = 1e-5
MASKED = -1e30


def layered_block_kernel(nc, x, attn_norm_w, ffn_norm_w, Wq, Wk, Wv, Wo, Wg, Wu, Wd, m_norm_w, Win, conv_w,
                         conv_b, Wx, A_log, Dp, Wout, gate_W, ln_scale, ln_bias, W1, b1, W2, b2, out):
    B, T, D = x.shape
    HF = D // P
    NC = T // P
    NH, HD = 16, D // 16
    NKV = Wk.shape[2] // HD
    NL = Win.shape[0]
    NS = A_log.shape[2]
    KC = conv_w.shape[2]
    FF = Wg.shape[2]
    FT = -(-FF // P)
    FR = FF - (FT - 1) * P
    NE, _, EH = W1.shape
    ET = NE * EH // P
    G = NS // 2
    SCALE = float(HD) ** -0.5
    PRODUCTS = [(0, 0), (0, 1), (1, 0), (1, 1), (0, 2), (2, 0)]
    KR = len(PRODUCTS) * HD

    ctx = ExitStack()
    with ctx:
        def sb(name, shape, dt=F32):
            return ctx.enter_context(nc.sbuf_tensor(name, shape, dt))

        sems = []

        def sem(name):
            s = ctx.enter_context(nc.semaphore(name))
            sems.append(s)
            return s

        win = sb("win", [P, NL, HF, 2 * D])
        wxd = sb("wxd", [P, NL, HF, D + 2 * NS])
        wxbc = sb("wxbc", [P, NL, HF, 3 * 2 * NS])
        wout = sb("wout", [P, NL, HF, D])
        wq = sb("wq", [P, HF, D])
        wk = sb("wk", [P, HF, P])
        wv = sb("wv", [P, HF, NKV * HD])
        wo = sb("wo", [P, NKV, D])
        wg = sb("wg", [P, HF, FF])
        wu = sb("wu", [P, HF, FF])
        wd = sb("wd", [P, FT, D])
        w1 = sb("w1", [P, HF, NE * EH])
        w2 = sb("w2", [P, ET, D])
        b2r = sb("b2r", [NE, D])
        gwt = sb("gwt", [P, HF, NE])
        anw = sb("anw", [P, HF])
        fnw = sb("fnw", [P, HF])
        mnw = sb("mnw", [P, NL, HF])
        cw = sb("cw", [P, NL, HF, KC])
        cb = sb("cb", [P, NL, HF])
        dp = sb("dp", [P, NL, HF])
        aneg = sb("aneg", [P, NL, HF, NS])
        lns = sb("lns", [P, HF, NE])
        lnb = sb("lnb", [P, HF, NE])
        b1c = sb("b1c", [P, ET])
        ident = sb("ident", [P, P])
        identb = sb("identb", [P, P], BF16)
        mean_w = sb("mean_w", [P, P])
        maskq = sb("maskq", [P, P], BF16)
        maskk = sb("maskk", [P, P], BF16)
        selbc = sb("selbc", [3 * 2 * NS, 2 * NS, P], BF16)
        sele = sb("sele", [NE, NE * EH], BF16)
        rank_w = sb("rank_w", [P, NC, NE])
        epsc = sb("epsc", [P, 3])
        res = sb("res", [P, HF, T])
        tA = sb("tA", [P, HF, T])
        tB = sb("tB", [P, HF, T])
        rs = sb("rs", [P, T])
        xbp = sb("xbp", [P, HF, KC - 1 + T])
        delta = xbp[:, :, KC - 1:KC - 1 + T]
        sz = sb("sz", [P, HF, T])
        xc = sb("xc", [P, HF, T])
        bcs = sb("bcs", [3 * 2 * NS, T], BF16)
        bcr = rs[0:4 * NS, :]
        decay = [sb(f"decay{k}", [P, HF, 2, T]) for k in range(2)]
        state = [sb(f"state{k}", [P, HF, 2, T]) for k in range(3)]
        cs = [sb(f"cs{k}", [P, 2, T]) for k in range(2)]
        hid = decay[0]
        x0t = cs[0]
        lg = sb("lg", [P, NC, NE])
        lmx = sb("lmx", [P, NC, 1])
        oh = sb("oh", [P, NC, NE])
        oht = sz[0:NE, 0, :]
        ohtb = sz[:, 1, :].bitcast(BF16)[0:NE, 0:T]
        hres = sb("hres", [P, HF, T])
        hA = sb("hA", [P, HF, T])
        xio = hA[:].rearrange("p h t -> p (h t)").rearrange("p (c d) -> p c d", c=NC)
        hxn = sb("hxn", [P, HF, T])
        x0h = hxn
        hrs = sb("hrs", [P, T])
        parts = sb("parts", [P, 3, HF + 1, T], BF16)
        of = parts[:].rearrange("p a h t -> p (a h t)").bitcast(F32)[:, 0:NKV * T].rearrange(
            "p (g t) -> p g t", g=NKV)
        qst = sb("qst", [KR + 1, NH, T], BF16)
        kst = sb("kst", [KR + 1, NKV, T], BF16)
        vp = sb("vp", [P, NC, NKV, 2 * HD])
        prob = sb("prob", [P, 4 * (2 * T - P)])
        rest = prob[:, 0:3 * T].rearrange("p (h t) -> p h t", t=T)
        mx = sb("mx", [P, NC, NH])
        negm = parts[0:NH, 0, 0, :]
        qk_dram = nc.dram_tensor("qk_parts", [3, (HF + 1) * P, T], BF16).ap()
        x0_dram = nc.dram_tensor("x_by_feature", [B, P, HF * T], F32).ap()
        nm_dram = nc.dram_tensor("neg_max", [NH, T], BF16).ap()
        gb = prob[:, 0:FT * T].rearrange("p (m t) -> p m t", t=T)

        def prob_of(s):
            return prob[:, 4 * T:] if s % 2 else prob[:, 0:4 * T]

        def gate_tile(m):
            return gb[:, m, :]

        hb = ctx.enter_context(nc.psum_tensor("hb", [P, 3, T], F32))
        bb = ctx.enter_context(nc.psum_tensor("bb", [P, 2, T], F32))
        cbk = ctx.enter_context(nc.psum_tensor("cbk", [P, T], F32))
        yb = ctx.enter_context(nc.psum_tensor("yb", [P, 2, T], F32))

        half = lambda v: v.rearrange("(h p) -> p h", p=P)

        s_load = sem("s_load")
        s_zero = sem("s_zero")
        s_b1 = sem("s_b1")
        s_ae = sem("s_ae")
        s_dve0 = sem("s_dve0")
        s_pool0 = sem("s_pool0")
        loads = [
            (win[:], Win.rearrange("l (h p) n -> p l h n", p=P)),
            (wxd[:], Wx.rearrange("l (h p) n -> p l h n", p=P)),
            (wout[:], Wout.rearrange("l (h p) n -> p l h n", p=P)),
            (wq[:], Wq[0].rearrange("(h p) n -> p h n", p=P)),
            (wk[:, :, 0:P // 2], Wk[0].rearrange("(h p) n -> p h n", p=P)),
            (wk[:, :, P // 2:P], Wk[0].rearrange("(h p) n -> p h n", p=P)),
            (wv[:], Wv[0].rearrange("(h p) n -> p h n", p=P)),
            (wg[:], Wg[0].rearrange("(h p) n -> p h n", p=P)),
            (wu[:], Wu[0].rearrange("(h p) n -> p h n", p=P)),
            (wd[:, 0:FT - 1, :], Wd[0, 0:(FT - 1) * P].rearrange("(m p) n -> p m n", p=P)),
            (wd[0:FR, FT - 1, :], Wd[0, (FT - 1) * P:FF]),
            (w2[:], W2.rearrange("(m a) h n -> (a h) m n", a=P // EH)),
            (b2r[:], b2),
            (anw[:], half(attn_norm_w[0])),
            (fnw[:], half(ffn_norm_w[0])),
            (b1c[:], b1.rearrange("(m a) h -> (a h) m", a=P // EH)),
        ]
        for h in range(HF):
            rows = slice(h * P, h * P + P)
            loads += [
                (w1[:, h, :].rearrange("p (e n) -> p e n", e=NE), W1[:, rows, :].rearrange("e p n -> p e n")),
                (gwt[:, h, :], gate_W[:, rows].rearrange("e p -> p e")),
                (lns[:, h, :], ln_scale[:, rows].rearrange("e p -> p e")),
                (lnb[:, h, :], ln_bias[:, rows].rearrange("e p -> p e")),
                (mnw[:, :, h], m_norm_w[:, rows].rearrange("l p -> p l")),
                (cw[:, :, h, :], conv_w[:, rows, :].rearrange("l p k -> p l k")),
                (cb[:, :, h], conv_b[:, rows].rearrange("l p -> p l")),
                (dp[:, :, h], Dp[:, rows].rearrange("l p -> p l")),
                (aneg[:, :, h, :], A_log[:, rows, :].rearrange("l p n -> p l n")),
            ]

        for j in range(4):
            loads.append((wo[32 * j:32 * j + HD], Wo[0].rearrange("(g j i) n -> j i g n", j=4, i=HD)[j]))

        with nc.Block() as block:
            @block.sync
            def _(sp):
                sp.wait_ge(s_zero, 1)
                for dst, src in loads:
                    with nc.allow_non_contiguous_dma(reason="small columns, once"):
                        sp.dma_start(dst, src).then_inc(s_load, 16)

            @block.gpsimd
            def _(pool):
                count = [0]

                def link(ins):
                    count[0] += 1
                    ins.then_inc(s_pool0, 1)
                    pool.wait_ge(s_pool0, count[0])

                def select(t, fill, cond, base, pattern, row):
                    link(pool.affine_select(out=t, in_=t, compare_op=cond, fill=fill, base=base,
                                            pattern=pattern, channel_multiplier=row))

                for t in (ident, identb, maskq, maskk, selbc, sele):
                    link(pool.memset(t[:], 0.0))
                select(ident[:], 1.0, ALU.not_equal, 0, [[-1, P]], 1)
                select(identb[:], 1.0, ALU.not_equal, 0, [[-1, P]], 1)
                select(maskq[:], MASKED, ALU.is_ge, 0, [[-1, P]], 1)
                select(maskk[:], MASKED, ALU.is_ge, 0, [[1, P]], -1)
                for part in range(3):
                    select(selbc[:], 1.0, ALU.not_equal, -2 * NS * part, [[-1, 2 * NS], [0, P]], 1)
                select(sele[:].rearrange("e (a n) -> e a n", a=NE), 1.0, ALU.not_equal, 0,
                       [[-1, NE], [0, EH]], 1)
                link(pool.memset(mean_w[:], 1.0 / D))

            @block.scalar
            def _(act):
                act.wait_ge(s_load, 16 * len(loads))
                act.activation(aneg[:], aneg[:], ACT.Exp).then_inc(s_ae, 1)

            @block.tensor
            def _(pe):
                pe.wait_ge(s_load, 16 * len(loads))
                for m in range(ET):
                    for h in range(HF):
                        last = pe.matmul(cbk[:, m * NE:(m + 1) * NE], w1[:, h, m * P:(m + 1) * P],
                                         lnb[:, h, :], start=(h == 0), stop=(h == HF - 1))
                last.then_inc(s_b1, 1)

            @block.vector
            def _(dve):
                count = [0]

                def link(ins):
                    count[0] += 1
                    ins.then_inc(s_dve0, 1)
                    dve.wait_ge(s_dve0, count[0])

                for k in range(3):
                    dve.memset(epsc[:, k:k + 1], (EPS_RMS, EPS_LN, 1.0)[k])
                for e in range(NE):
                    dve.memset(rank_w[:, :, e], float(NE - e))
                for k in range(2):
                    dve.memset(decay[k][:, :, :, 0:1], 0.0)
                dve.memset(xbp[:, :, 0:KC - 1], 0.0)
                dve.memset(wo[:], 0.0).then_inc(s_zero, 1)
                dve.memset(vp[:, :, :, HD:2 * HD], 1.0)
                dve.memset(kst[KR:KR + 1, :, :], 1.0)
                dve.wait_ge(s_load, 16 * len(loads))
                for h in range(HF):
                    for w, c in ((wq, anw), (wk, anw), (wv, anw), (wg, fnw), (wu, fnw)):
                        link(dve.tensor_scalar(w[:, h, :], w[:, h, :], c[:, h:h + 1], None, ALU.mult))
                    for l in range(NL):
                        link(dve.tensor_scalar(win[:, l, h, :], win[:, l, h, :], mnw[:, l, h:h + 1], None,
                                               ALU.mult))
                for k in range(3):
                    dve.tensor_copy(wxbc[:, :, :, k * 2 * NS:(k + 1) * 2 * NS], wxd[:, :, :, D:D + 2 * NS])
                dve.wait_ge(s_ae, 1)
                dve.tensor_scalar(aneg[:], aneg[:], -1.0, None, ALU.mult)
                dve.wait_ge(s_b1, 1)
                for m in range(ET):
                    for a in range(P // EH):
                        rows = slice(a * EH, (a + 1) * EH)
                        e = m * (P // EH) + a
                        dve.tensor_tensor(b1c[rows, m:m + 1], b1c[rows, m:m + 1],
                                          cbk[rows, m * NE + e:m * NE + e + 1], ALU.add)
                for h in range(HF):
                    for e in range(NE):
                        dve.tensor_scalar(w1[:, h, e * EH:(e + 1) * EH], w1[:, h, e * EH:(e + 1) * EH],
                                          lns[:, h, e:e + 1], None, ALU.mult)

        setup_sems = len(sems)
        t_own = sem("t_own")
        t_res = sem("t_res")
        t_sq = sem("t_sq")
        t_stat = sem("t_stat")
        t_ln = sem("t_ln")
        t_rs = sem("t_rs")
        t_cen = sem("t_cen")
        t_xn = sem("t_xn")
        t_xb = sem("t_xb")
        t_z = sem("t_z")
        t_xbp = sem("t_xbp")
        t_conv = sem("t_conv")
        t_xc = sem("t_xc")
        t_bc = sem("t_bc")
        t_dl = sem("t_dl")
        t_split = sem("t_split")
        t_abs = sem("t_abs")
        t_delta = sem("t_delta")
        t_u = sem("t_u")
        b_ready = sem("b_ready")
        b_used = sem("b_used")
        c_ready = sem("c_ready")
        c_copied = sem("c_copied")
        decay_ready = sem("decay_ready")
        scanned = sem("scanned")
        p_own = sem("p_own")
        weighed = sem("weighed")
        summed = sem("summed")
        t_yg = sem("t_yg")
        t_out = sem("t_out")
        e_x0 = sem("e_x0")
        e_lg = sem("e_lg")
        e_oh = sem("e_oh")
        e_oht = sem("e_oht")
        e_ohc = sem("e_ohc")
        e_hp = sem("e_hp")
        e_mask = sem("e_mask")
        e_gelu = sem("e_gelu")
        e_hm = sem("e_hm")
        e_w2 = sem("e_w2")
        e_fin = sem("e_fin")
        e_ft = sem("e_ft")
        e_fc = sem("e_fc")
        e_store = sem("e_store")

        h_x = sem("h_x")
        h_tr = sem("h_tr")
        h_x0 = sem("h_x0")
        h_cen = sem("h_cen")
        h_x0w = sem("h_x0w")
        h_sq = sem("h_sq")
        h_stat = sem("h_stat")
        h_ln = sem("h_ln")
        h_rs = sem("h_rs")
        h_xn = sem("h_xn")
        h_q = sem("h_q")
        h_hi = sem("h_hi")
        h_lo1 = sem("h_lo1")
        h_mid = sem("h_mid")
        h_lo2 = sem("h_lo2")
        h_qkw = sem("h_qkw")
        h_qks = sem("h_qks")
        h_v = sem("h_v")
        h_vp = sem("h_vp")
        h_s = sem("h_s")
        h_mx = sem("h_mx")
        h_mt = sem("h_mt")
        h_nm = sem("h_nm")
        h_nmw = sem("h_nmw")
        h_nms = sem("h_nms")
        h_st = sem("h_st")
        h_p = sem("h_p")
        h_pv = sem("h_pv")
        h_dl = sem("h_dl")
        h_ri = sem("h_ri")
        h_rw = sem("h_rw")
        h_on = sem("h_on")
        h_wo = sem("h_wo")
        h_r2 = sem("h_r2")
        h_g = sem("h_g")
        h_gc = sem("h_gc")
        h_si = sem("h_si")
        h_u = sem("h_u")
        h_h = sem("h_h")
        h_wd = sem("h_wd")

        MAXB = [[(0, 0), (P, 2)], [(0, 3)], [(0, 1)]]
        EXPB = [[[0], [1], [2], [3]], [[0], [1], [2], [3]], [[0, 1], [2, 3]], [[0, 1, 2, 3]]]
        EXPN = [len(b) for b in EXPB]
        NB = 3

        def exp_unit(s):
            return sum(EXPN) * (s // NC) + sum(EXPN[0:s % NC])

        PL = G + 4
        POINTS = NL * PL + 6
        BESIDE = {0: ["load"], 1: ["centre"], 2: ["var"], 3: ["scale"], 4: ["ms"], 5: ["norm"], 6: ["qk"],
                  7: ["mid"], 8: ["v"], 18: ["maxrow"], 36: ["last"], 37: ["wo"], 38: ["fms"], 39: ["fnorm"],
                  40: ["gate"], 41: ["up", "down"]}
        for n in range(8):
            BESIDE[10 + n] = [("max", 2 * n), ("max", 2 * n + 1)]
        for n in range(NH):
            BESIDE[20 + n] = [("attend", n)]

        def turn(head, tail):
            do_h, do_t = head is not None, tail is not None

            def beside(point, steps):
                if do_h:
                    for what in BESIDE.get(point, []):
                        name, *which = (what,) if isinstance(what, str) else what
                        if name in steps:
                            steps[name](*which)

            def sp_program(sp):
                if do_h:
                    sp.dma_start(xio, x[bass.ds(head, 1)].rearrange("b (c p) d -> p (b c) d", p=P)
                                 ).then_inc(h_x, 16)
                    sp.wait_ge(h_x0, 1)
                    sp.dma_start(x0_dram[bass.ds(head, 1)].rearrange("b p t -> (b p) t"),
                                 x0h[:].rearrange("p h t -> p (h t)")).then_inc(h_x0w, 16)
                    sp.wait_ge(h_x0w, 16)
                    sp.wait_ge(h_lo2, 1)
                    sp.dma_start(qk_dram.rearrange("a (h p) t -> p a h t", p=P), parts[:]).then_inc(h_qkw, 16)
                    sp.wait_ge(h_qkw, 16)
                    for n, (kpart, qpart) in enumerate(PRODUCTS):
                        rows = slice(n * HD, (n + 1) * HD)
                        sp.dma_start(qst[rows], qk_dram[qpart, 0:D].rearrange("(h j) t -> j h t", j=HD)
                                     ).then_inc(h_qks, 16)
                        sp.dma_start(kst[rows], qk_dram[kpart, D:D + NKV * HD].rearrange(
                            "(h j) t -> j h t", j=HD)).then_inc(h_qks, 16)
                    sp.wait_ge(h_nm, 1)
                    sp.dma_start(nm_dram, negm).then_inc(h_nmw, 16)
                    sp.wait_ge(h_nmw, 16)
                    sp.dma_start(qst[KR:KR + 1].rearrange("o h t -> o (h t)"),
                                 nm_dram.rearrange("(o h) t -> o (h t)", o=1)).then_inc(h_nms, 16)
                if do_t:
                    sp.wait_ge(weighed, HF * G * NL)
                    sp.dma_start(x0t[:].rearrange("p h t -> p (h t)"),
                                 x0_dram[bass.ds(tail, 1)].rearrange("b p t -> (b p) t")).then_inc(e_x0, 16)
                    sp.wait_ge(e_fc, 2)
                    sp.dma_start(out[bass.ds(tail, 1)].rearrange("b (c p) d -> p (b c) d", p=P),
                                 state[0][:].rearrange("p h n t -> p (h n t)")[:, 0:NC * D]
                                 .rearrange("p (c d) -> p c d", c=NC)).then_inc(e_store, 16)
                    sp.wait_ge(e_store, 16)

            def pe_program(pe):
                def project(dst, w, src, cols, n=P, stop=True):
                    for h in range(HF):
                        last = pe.matmul(dst, w[:, h, cols:cols + n], src[:, h, :], start=(h == 0),
                                         stop=(h == HF - 1))
                    return last

                def stat(dst, src):
                    for h in range(HF):
                        last = pe.matmul(dst, mean_w[:], src[:, h, :], start=(h == 0), stop=(h == HF - 1))
                    return last

                def pre(l):
                    wl, xl = win[:, l], wxd[:, l]
                    pe.wait_ge(t_sq, l + 1)
                    stat(yb[:, 0, :], tA).then_inc(t_stat, 1)
                    beside(PL * l, steps)
                    pe.wait_ge(t_xn, l + 1)
                    for j in range(2):
                        last = project(bb[:, j, :], wl, tB, j * P)
                    last.then_inc(t_xb, 1)
                    project(cbk[:], wl, tB, 2 * P)
                    project(yb[:, 1, :], wl, tB, 3 * P).then_inc(t_z, 1)

                def pre_x(l):
                    pe.wait_ge(t_xc, l + 1)
                    project(cbk[0:3 * 2 * NS, :], wxbc[:, l], xc, 0, 3 * 2 * NS).then_inc(t_bc, 1)
                    for j in range(2):
                        last = project(bb[:, j, :], wxd[:, l], xc, j * P)
                    last.then_inc(t_dl, 1)

                def spread(l, g):
                    k = G * l + g
                    if g == 0:
                        pe.wait_ge(t_split, l + 1)
                        pe.wait_ge(t_delta, l + 1)
                    for j in range(2):
                        n = 2 * g + j
                        if g > 0:
                            pe.wait_ge(b_used, 2 * (k - 1) + j + 1)
                        pe.matmul(bb[:, j, :], selbc[:, n, :], bcs[:], start=True, stop=True
                                  ).then_inc(b_ready, 1)
                        if n > 0:
                            pe.wait_ge(c_copied, 2 * k + j)
                        pe.matmul(cbk[:], selbc[:, NS + n, :], bcs[:], start=True, stop=True
                                  ).then_inc(c_ready, 1)

                def sum_states(l, g):
                    k = G * l + g
                    for h in range(HF):
                        pe.wait_ge(weighed, HF * k + h + 1)
                        last = pe.matmul(yb[:, h, :], ident[:], state[k % 3][:, h, 0, :],
                                         start=(g == 0), stop=(g == G - 1))
                    last.then_inc(summed, 1)

                def post(l):
                    pe.wait_ge(t_yg, l + 1)
                    for j in range(2):
                        last = project(bb[:, j, :], wout[:, l], tA, j * P)
                    last.then_inc(t_out, 1)

                def experts_norm():
                    pe.wait_ge(t_res, NL + 2)
                    stat(yb[:, 0, :], x0t).then_inc(t_stat, 1)
                    beside(PL * NL, steps)
                    pe.wait_ge(t_sq, NL + 1)
                    stat(yb[:, 1, :], tA).then_inc(t_stat, 1)
                    beside(PL * NL + 1, steps)
                    pe.wait_ge(t_xn, NL + 1)
                    for c in range(NC):
                        for h in range(HF):
                            last = pe.matmul(cbk[:, c * NE:(c + 1) * NE], tB[:, h, c * P:(c + 1) * P],
                                             gwt[:, h, :], start=(h == 0), stop=(h == HF - 1))
                    last.then_inc(e_lg, 1)
                    pe.wait_ge(t_sq, NL + 2)
                    stat(yb[:, 0, :], tA).then_inc(t_stat, 1)

                def experts():
                    beside(PL * NL + 2, steps)
                    pe.wait_ge(e_oh, 1)
                    for c in range(NC):
                        last = pe.transpose(cbk[0:NE, c * P:(c + 1) * P], oh[:, c, :], ident[:])
                    last.then_inc(e_oht, 1)
                    beside(PL * NL + 3, steps)
                    pe.wait_ge(t_xn, NL + 2)
                    for m in range(ET):
                        if m >= 2:
                            pe.wait_ge(e_gelu, m - 1)
                        project(bb[:, m % 2, :], w1, tB, m * P).then_inc(e_hp, 1)
                        if m == 0:
                            pe.wait_ge(e_ohc, 1)
                        if m >= 2:
                            pe.wait_ge(e_hm, m - 1)
                        pe.matmul(yb[:, m % 2, :], sele[:, m * P:(m + 1) * P], ohtb, start=True,
                                  stop=True).then_inc(e_mask, 1)
                    beside(PL * NL + 4, steps)
                    pe.wait_ge(e_hm, ET)
                    for j in range(2):
                        for m in range(ET):
                            pe.matmul(bb[:, j, :], w2[:, m, j * P:(j + 1) * P],
                                      hid[:, m // 2, m % 2, :], start=(m == 0), stop=False)
                        last = pe.matmul(bb[:, j, :], b2r[:, j * P:(j + 1) * P], oht, start=False, stop=True)
                    last.then_inc(e_w2, 1)
                    beside(PL * NL + 5, steps)
                    pe.wait_ge(e_fin, 1)
                    for b in range(2):
                        for c in range(2):
                            for h in range(HF):
                                last = pe.transpose(yb[:, b, c * D + h * P:c * D + h * P + P],
                                                    tA[:, h, (2 * b + c) * P:(2 * b + c + 1) * P], ident[:])
                        last.then_inc(e_ft, 1)

                def h_load():
                    pe.wait_ge(h_x, 16)
                    for h in range(HF):
                        for c in range(NC):
                            last = pe.transpose(hb[:, h, c * P:(c + 1) * P], xio[:, c, h * P:(h + 1) * P],
                                                ident[:])
                    last.then_inc(h_tr, 1)

                def h_mean():
                    pe.wait_ge(h_x0, 1)
                    stat(hb[:, 2, :], x0h).then_inc(h_stat, 1)

                def h_norm(m, bank):
                    pe.wait_ge(h_sq, m)
                    stat(hb[:, bank, :], hxn).then_inc(h_stat, 1)

                def h_qk():
                    pe.wait_ge(h_xn, 1)
                    for j in range(2):
                        project(hb[:, j, :], wq, hxn, j * P)
                    project(hb[:, 2, :], wk, hxn, 0).then_inc(h_q, 1)

                def h_values():
                    pe.wait_ge(h_lo2, 1)
                    for c in range(NC):
                        for h in range(HF):
                            last = pe.matmul(hb[:, 0, c * 64:(c + 1) * 64], hxn[:, h, c * P:(c + 1) * P],
                                             wv[:, h, :], start=(h == 0), stop=(h == HF - 1))
                    last.then_inc(h_v, 1)

                def h_max(h):
                    if h == 0:
                        pe.wait_ge(h_vp, 1)
                        pe.wait_ge(h_qks, 32 * len(PRODUCTS))
                    for b in range(NB):
                        if h > 0:
                            pe.wait_ge(h_mx, NB * (h - 1) + b + 1)
                        for col, c in MAXB[b]:
                            n = (c + 1) * P
                            pe.matmul(hb[:, b, col:col + n], qst[0:KR, h, c * P:n], kst[0:KR, h // 4, 0:n],
                                      start=True, stop=False)
                            last = pe.matmul(hb[:, b, col + n - P:col + n], identb[:], maskq[:],
                                             start=False, stop=True)
                        last.then_inc(h_s, 1)

                def h_maxrow():
                    pe.wait_ge(h_mx, NB * NH)
                    for c in range(NC):
                        last = pe.transpose(hb[0:NH, 0, c * P:(c + 1) * P], mx[:, c, :], ident[:])
                    last.then_inc(h_mt, 1)

                def h_attend(s):
                    a, c = divmod(s, NC)
                    n = T - c * P
                    if s == 0:
                        pe.wait_ge(h_nms, 16)
                    for b, heads in enumerate(EXPB[c]):
                        w = exp_unit(s) + b
                        if w >= 2:
                            pe.wait_ge(h_p, w - 1)
                        for i, j in enumerate(heads):
                            pe.matmul(hb[:, w % 2, i * n:(i + 1) * n], kst[:, a, c * P:(c + 1) * P],
                                      qst[:, 4 * a + j, c * P:T], start=True, stop=False)
                            last = pe.matmul(hb[:, w % 2, i * n:i * n + P], identb[:], maskk[:], start=False,
                                             stop=True)
                        last.then_inc(h_st, 1)
                    if s > 0:
                        h_weigh(s - 1)

                def h_weigh(s):
                    a, c = divmod(s, NC)
                    n = T - c * P
                    pe.wait_ge(h_p, exp_unit(s + 1))
                    if c == 0 and a > 0:
                        pe.wait_ge(h_on, a)
                    v = prob_of(s)
                    for j in range(4):
                        last = pe.matmul(hb[32 * j:32 * j + 32, 2, c * P:T], vp[:, c, a, :],
                                         v[:, j * n:(j + 1) * n], start=(c == 0), stop=(c == NC - 1))
                    last.then_inc(h_pv, 1)

                def h_attn_out():
                    pe.wait_ge(h_on, NKV)
                    for j in range(2):
                        for a in range(NKV):
                            last = pe.matmul(hb[:, j, :], wo[:, a, j * P:(j + 1) * P], of[:, a, :],
                                             start=(a == 0), stop=(a == NKV - 1))
                    last.then_inc(h_wo, 1)

                def h_ffn_gate():
                    pe.wait_ge(h_xn, 2)
                    for m in range(FT):
                        n = P if m < FT - 1 else FR
                        if m >= 3:
                            pe.wait_ge(h_gc, m - 2)
                        project(hb[0:n, m % 3, :], wg, hxn, m * P, n).then_inc(h_g, 1)

                def h_ffn_up():
                    for m in range(FT):
                        n = P if m < FT - 1 else FR
                        pe.wait_ge(h_gc, m + 4 if m < 3 else FT)
                        if m >= 3:
                            pe.wait_ge(h_h, m - 2)
                        project(hb[0:n, m % 3, :], wu, hxn, m * P, n).then_inc(h_u, 1)

                def h_ffn_down():
                    pe.wait_ge(h_h, FT)
                    for j in range(2):
                        for m in range(FT):
                            n = P if m < FT - 1 else FR
                            last = pe.matmul(hb[:, j, :], wd[0:n, m, j * P:(j + 1) * P], gate_tile(m)[0:n],
                                             start=(m == 0), stop=(m == FT - 1))
                    last.then_inc(h_wd, 1)

                steps = {"load": h_load, "centre": h_mean, "var": lambda: h_norm(1, 0), "ms": lambda: h_norm(2, 1),
                         "qk": h_qk, "v": h_values, "max": h_max, "maxrow": h_maxrow, "attend": h_attend,
                         "last": lambda: h_weigh(NH - 1), "wo": h_attn_out, "fms": lambda: h_norm(3, 2),
                         "gate": h_ffn_gate, "up": h_ffn_up, "down": h_ffn_down}
                if do_t:
                    for l in range(NL):
                        pre(l)
                        beside(PL * l + 1, steps)
                        pre_x(l)
                        beside(PL * l + 2, steps)
                        spread(l, 0)
                        for g in range(G):
                            if g < G - 1:
                                spread(l, g + 1)
                            beside(PL * l + 3 + g, steps)
                            if g > 0:
                                sum_states(l, g - 1)
                        sum_states(l, G - 1)
                        beside(PL * l + 3 + G, steps)
                        post(l)
                    experts_norm()
                    experts()
                else:
                    for point in range(POINTS):
                        beside(point, steps)

            def act_program(act):
                def exp_and_log():
                    act.preload_act_table_set("natural_log_exp_and_others")

                def root(dst, src, eps, ln, rs_sem, n):
                    act.activation(dst, src, ACT.Ln, bias=epsc[:, eps:eps + 1]).then_inc(ln, 1)
                    act.wait_ge(ln, n)
                    act.activation(dst, dst, ACT.Exp, scale=-0.5).then_inc(rs_sem, 1)

                def pre(l):
                    act.wait_ge(t_res, l + 1)
                    act.activation(tA[:], res[:], ACT.Square).then_inc(t_sq, 1)
                    act.wait_ge(t_stat, l + 1)
                    root(rs[:], yb[:, 0, :], 0, t_ln, t_rs, l + 1)
                    beside(PL * l, steps)
                    act.wait_ge(t_xb, l + 1)
                    act.activation(xbp[:, :, KC - 1:KC - 1 + T], bb[:], ACT.Copy).then_inc(t_xbp, 1)
                    act.wait_ge(t_z, l + 1)
                    act.activation(sz[:, 0, :], cbk[:], ACT.Silu)
                    act.activation(sz[:, 1, :], yb[:, 1, :], ACT.Silu)
                    act.wait_ge(t_conv, l + 1)
                    act.activation(xc[:], tA[:], ACT.Silu).then_inc(t_xc, 1)
                    exp_and_log()

                def softplus(l):
                    act.wait_ge(t_dl, l + 1)
                    act.activation(tA[:], bb[:], ACT.Abs).then_inc(t_abs, 1)
                    act.wait_ge(t_abs, 3 * l + 1)
                    act.activation(tA[:], tA[:], ACT.Exp, scale=-1.0).then_inc(t_abs, 1)
                    act.wait_ge(t_abs, 3 * l + 2)
                    act.activation(tA[:], tA[:], ACT.Ln, bias=epsc[:, 2:3]).then_inc(t_abs, 1)

                def step(l, g):
                    k = G * l + g
                    if g == 0:
                        act.wait_ge(t_delta, l + 1)
                    for j in range(2):
                        if k >= 2:
                            act.wait_ge(weighed, HF * (k - 1))
                        act.wait_ge(c_ready, 2 * k + j + 1)
                        act.activation(cs[k % 2][:, j, :], cbk[:], ACT.Copy).then_inc(c_copied, 1)
                    if k >= 2:
                        act.wait_ge(scanned, k - 1)
                    for h in range(HF):
                        for j in range(2):
                            last = act.activation(decay[k % 2][:, h, j, 1:T], delta[:, h, 1:T], ACT.Exp,
                                                  scale=aneg[:, l, h, 2 * g + j:2 * g + j + 1])
                    last.then_inc(decay_ready, 1)

                def experts_norm():
                    beside(PL * NL, steps)
                    act.wait_ge(t_cen, 1)
                    act.activation(tA[:], tB[:], ACT.Square).then_inc(t_sq, 1)
                    act.wait_ge(t_stat, NL + 2)
                    root(rs[:], yb[:, 1, :], 1, t_ln, t_rs, NL + 1)
                    beside(PL * NL + 1, steps)
                    act.wait_ge(t_xn, NL + 1)
                    act.activation(tA[:], tB[:], ACT.Square).then_inc(t_sq, 1)
                    act.wait_ge(t_stat, NL + 3)
                    root(rs[:], yb[:, 0, :], 1, t_ln, t_rs, NL + 2)

                def experts():
                    beside(PL * NL + 2, steps)
                    act.wait_ge(e_oht, 1)
                    act.activation(oht, cbk[0:NE, :], ACT.Copy)
                    act.activation(ohtb, cbk[0:NE, :], ACT.Copy).then_inc(e_ohc, 1)
                    beside(PL * NL + 3, steps)
                    for m in range(ET):
                        act.wait_ge(e_hp, m + 1)
                        act.activation(hid[:, m // 2, m % 2, :], bb[:, m % 2, :], ACT.Gelu,
                                       bias=b1c[:, m:m + 1]).then_inc(e_gelu, 1)
                    exp_and_log()
                    beside(PL * NL + 4, steps)
                    beside(PL * NL + 5, steps)
                    fin = state[0][:].rearrange("p h n t -> p (h n t)")
                    for b in range(2):
                        act.wait_ge(e_ft, b + 1)
                        act.activation(fin[:, b * 2 * D:(b + 1) * 2 * D], yb[:, b, :], ACT.Copy
                                       ).then_inc(e_fc, 1)

                def h_load():
                    act.wait_ge(h_tr, 1)
                    act.activation(x0h[:], hb[:, 0:2, :], ACT.Copy).then_inc(h_x0, 1)

                def h_square(src):
                    act.wait_ge(h_x0w, 16)
                    act.activation(hxn[:], src, ACT.Square).then_inc(h_sq, 1)

                def h_root(m, bank, eps):
                    act.wait_ge(h_stat, m + 1)
                    root(hrs[:], hb[:, bank, :], eps, h_ln, h_rs, m)

                def h_var():
                    act.wait_ge(h_cen, 1)
                    h_square(hA[:])

                def h_ms():
                    act.wait_ge(h_cen, 2)
                    h_square(hres[:])

                def h_first():
                    act.wait_ge(h_q, 1)
                    act.activation(parts[:, 0], hb[:], ACT.Copy).then_inc(h_hi, 1)

                def h_mid_():
                    act.wait_ge(h_lo1, 1)
                    act.activation(parts[:, 1], rest, ACT.Copy).then_inc(h_mid, 1)

                def h_values():
                    act.wait_ge(h_v, 1)
                    act.activation(vp[:, :, :, 0:HD], hb[:, 0, 0:NC * 64].rearrange(
                        "p (c g j) -> p c g j", c=NC, g=NKV), ACT.Copy).then_inc(h_vp, 1)

                def h_negmax():
                    act.wait_ge(h_mt, 1)
                    act.activation(negm, hb[0:NH, 0, :], ACT.Copy, scale=-1.0).then_inc(h_nm, 1)

                def h_probs(s):
                    c = s % NC
                    n = T - c * P
                    if s >= 2:
                        act.wait_ge(h_pv, s - 1)
                    v = prob_of(s)
                    for b, heads in enumerate(EXPB[c]):
                        w = exp_unit(s) + b
                        act.wait_ge(h_st, w + 1)
                        act.activation(v[:, heads[0] * n:(heads[-1] + 1) * n], hb[:, w % 2, 0:len(heads) * n],
                                       ACT.Exp, scale=SCALE).then_inc(h_p, 1)
                    if c == 0 and s > 0:
                        h_inv(s // NC - 1)

                def h_inv(a):
                    act.wait_ge(h_pv, NC * (a + 1))
                    if a > 0:
                        act.wait_ge(h_rw, a)
                    act.activation(hrs[:], hb[:, 2, :], ACT.Abs).then_inc(h_dl, 1)
                    act.wait_ge(h_dl, 2 * a + 1)
                    act.activation(hrs[:], hrs[:], ACT.Ln).then_inc(h_dl, 1)
                    act.wait_ge(h_dl, 2 * a + 2)
                    act.activation(hrs[:], hrs[:], ACT.Exp, scale=-1.0).then_inc(h_ri, 1)

                def h_fms():
                    act.wait_ge(h_r2, 1)
                    h_square(hres[:])

                def h_gate():
                    for m in range(FT):
                        n = P if m < FT - 1 else FR
                        act.wait_ge(h_g, m + 1)
                        act.activation(gate_tile(m)[0:n], hb[0:n, m % 3, :], ACT.Copy).then_inc(h_gc, 1)
                    act.wait_ge(h_gc, FT)
                    act.activation(gb[:, 0:FT - 1], gb[:, 0:FT - 1], ACT.Silu)
                    act.activation(gb[0:FR, FT - 1], gb[0:FR, FT - 1], ACT.Silu).then_inc(h_si, 1)
                    exp_and_log()

                steps = {"load": h_load, "var": h_var, "scale": lambda: h_root(1, 0, 1), "ms": h_ms,
                         "norm": lambda: h_root(2, 1, 0), "qk": h_first, "mid": h_mid_, "v": h_values,
                         "maxrow": h_negmax, "attend": h_probs, "last": lambda: h_inv(NKV - 1), "fms": h_fms,
                         "fnorm": lambda: h_root(3, 2, 0), "gate": h_gate}
                exp_and_log()
                if do_t:
                    for l in range(NL):
                        pre(l)
                        beside(PL * l + 1, steps)
                        softplus(l)
                        beside(PL * l + 2, steps)
                        step(l, 0)
                        for g in range(G):
                            if g < G - 1:
                                step(l, g + 1)
                            beside(PL * l + 3 + g, steps)
                        beside(PL * l + 3 + G, steps)
                    experts_norm()
                    experts()
                else:
                    for point in range(POINTS):
                        beside(point, steps)

            def dve_program(dve):
                own = [0]

                def link(ins):
                    own[0] += 1
                    ins.then_inc(t_own, 1)
                    dve.wait_ge(t_own, own[0])

                def over_halves(v, n=HF):
                    return v.rearrange("p (a t) -> p a t", a=1).broadcast_to([P, n, T])

                def take():
                    dve.tensor_copy(res[:], hres[:]).then_inc(t_res, 1)

                def pre(l):
                    dve.wait_ge(t_rs, l + 1)
                    dve.tensor_tensor(tB[:], res[:], over_halves(rs[:]), ALU.mult).then_inc(t_xn, 1)
                    beside(PL * l, steps)

                def conv(l):
                    dve.wait_ge(t_xbp, l + 1)
                    for h in range(HF):
                        last = dve.tensor_scalar(tA[:, h, :], xbp[:, h, 0:T], cw[:, l, h, 0:1],
                                                 cb[:, l, h:h + 1], ALU.mult, ALU.add)
                    for k in range(1, KC):
                        link(last)
                        for h in range(HF):
                            last = dve.scalar_tensor_tensor(out=tA[:, h, :], in0=xbp[:, h, k:k + T],
                                                            scalar=cw[:, l, h, k:k + 1], in1=tA[:, h, :],
                                                            op0=ALU.mult, op1=ALU.add)
                    last.then_inc(t_conv, 1)

                def split(l):
                    dve.wait_ge(t_bc, l + 1)
                    link(dve.tensor_copy(bcs[:], cbk[0:6 * NS, :]))
                    link(dve.tensor_tensor(bcr, cbk[0:4 * NS, :], bcs[0:4 * NS, :], ALU.subtract))
                    link(dve.tensor_copy(bcs[0:4 * NS, :], bcr))
                    dve.tensor_tensor(bcs[0:2 * NS, :], bcr[0:2 * NS, :], bcs[0:2 * NS, :],
                                      ALU.subtract).then_inc(t_split, 1)
                    dve.wait_ge(t_abs, 3 * l + 3)
                    dve.scalar_tensor_tensor(out=delta, in0=bb[:], scalar=0.0, in1=tA[:], op0=ALU.max,
                                             op1=ALU.add).then_inc(t_delta, 1)
                    dve.wait_ge(t_delta, l + 1)
                    dve.tensor_tensor(tB[:], delta, xc[:], ALU.mult).then_inc(t_u, 1)
                    dve.wait_ge(t_u, l + 1)

                def step(l, g):
                    k = G * l + g
                    if k >= 3:
                        dve.wait_ge(summed, k - 2)
                    for j in range(2):
                        dve.wait_ge(b_ready, 2 * k + j + 1)
                        dve.tensor_tensor(state[k % 3][:, :, j, :], tB[:], over_halves(bb[:, j, :]),
                                          ALU.mult).then_inc(b_used, 1)
                    dve.wait_ge(b_used, 2 * k + 2)
                    dve.wait_ge(decay_ready, k + 1)
                    flat = state[k % 3][:].rearrange("p h n t -> p (h n t)")
                    dve.tensor_tensor_scan(flat, decay[k % 2][:].rearrange("p h n t -> p (h n t)"), flat, 0.0,
                                           ALU.mult, ALU.add).then_inc(scanned, 1)

                def post(l):
                    dve.wait_ge(summed, G * (l + 1))
                    beside(PL * l + 3 + G, steps)
                    for h in range(HF):
                        last = dve.scalar_tensor_tensor(out=tA[:, h, :], in0=xc[:, h, :],
                                                        scalar=dp[:, l, h:h + 1], in1=yb[:, h, :],
                                                        op0=ALU.mult, op1=ALU.add)
                    link(last)
                    dve.tensor_tensor(tA[:], tA[:], sz[:], ALU.mult).then_inc(t_yg, 1)
                    dve.wait_ge(t_out, l + 1)
                    dve.tensor_tensor(res[:], res[:], bb[:], ALU.add).then_inc(t_res, 1)

                def experts_norm():
                    dve.wait_ge(e_x0, 16)
                    dve.wait_ge(t_res, NL + 1)
                    dve.tensor_tensor(x0t[:], x0t[:], res[:], ALU.add).then_inc(t_res, 1)
                    dve.wait_ge(t_stat, NL + 1)
                    dve.wait_ge(t_res, NL + 2)
                    dve.tensor_tensor(tB[:], x0t[:], over_halves(yb[:, 0, :]), ALU.subtract
                                      ).then_inc(t_cen, 1)
                    beside(PL * NL, steps)
                    dve.wait_ge(t_cen, 1)
                    dve.wait_ge(t_rs, NL + 1)
                    dve.tensor_tensor(tB[:], tB[:], over_halves(rs[:]), ALU.mult).then_inc(t_xn, 1)

                def experts_pick():
                    beside(PL * NL + 1, steps)
                    dve.wait_ge(e_lg, 1)
                    link(dve.tensor_copy(lg[:], cbk[:, 0:NC * NE].rearrange("p (c e) -> p c e", c=NC)))
                    link(dve.tensor_reduce(lmx[:], lg[:], AX.X, ALU.max))
                    link(dve.tensor_tensor(lg[:], lg[:], lmx[:].broadcast_to([P, NC, NE]), ALU.is_ge))
                    link(dve.tensor_tensor(lg[:], lg[:], rank_w[:], ALU.mult))
                    link(dve.tensor_reduce(lmx[:], lg[:], AX.X, ALU.max))
                    dve.tensor_tensor(oh[:], lg[:], lmx[:].broadcast_to([P, NC, NE]), ALU.is_equal
                                      ).then_inc(e_oh, 1)

                def experts():
                    beside(PL * NL + 2, steps)
                    dve.wait_ge(t_rs, NL + 2)
                    dve.tensor_tensor(tB[:], tB[:], over_halves(rs[:]), ALU.mult).then_inc(t_xn, 1)
                    beside(PL * NL + 3, steps)
                    for m in range(ET):
                        dve.wait_ge(e_gelu, m + 1)
                        dve.wait_ge(e_mask, m + 1)
                        v = hid[:, m // 2, m % 2, :]
                        dve.tensor_tensor(v, v, yb[:, m % 2, :], ALU.mult).then_inc(e_hm, 1)
                    beside(PL * NL + 4, steps)
                    dve.wait_ge(e_w2, 1)
                    dve.tensor_tensor(tA[:], x0t[:], bb[:], ALU.add).then_inc(e_fin, 1)
                    beside(PL * NL + 5, steps)
                    dve.memset(hid[:, :, :, 0:1], 0.0)

                def h_centre():
                    dve.wait_ge(h_stat, 1)
                    dve.tensor_tensor(hA[:], x0h[:], over_halves(hb[:, 2, :]), ALU.subtract).then_inc(h_cen, 1)

                def h_scale():
                    dve.wait_ge(h_cen, 1)
                    dve.wait_ge(h_rs, 1)
                    dve.tensor_tensor(hres[:], hA[:], over_halves(hrs[:]), ALU.mult).then_inc(h_cen, 1)

                def h_norm():
                    dve.wait_ge(h_cen, 2)
                    dve.wait_ge(h_rs, 2)
                    dve.tensor_tensor(hxn[:], hres[:], over_halves(hrs[:]), ALU.mult).then_inc(h_xn, 1)

                def h_rest():
                    dve.wait_ge(h_hi, 1)
                    dve.tensor_tensor(rest, hb[:], parts[:, 0], ALU.subtract).then_inc(h_lo1, 1)

                def h_third():
                    dve.wait_ge(h_mid, 1)
                    dve.tensor_tensor(parts[:, 2], rest, parts[:, 1], ALU.subtract).then_inc(h_lo2, 1)

                def h_max(h):
                    for b in range(NB):
                        dve.wait_ge(h_s, NB * h + b + 1)
                        for col, c in MAXB[b]:
                            last = dve.tensor_reduce(mx[:, c, h:h + 1], hb[:, b, col:col + (c + 1) * P], AX.X,
                                                     ALU.max)
                        last.then_inc(h_mx, 1)

                def h_normalise(a):
                    dve.wait_ge(h_ri, a + 1)
                    dve.stream_shuffle(hrs[:], hrs[:], [HD + i % HD for i in range(32)]).then_inc(h_rw, 1)
                    dve.wait_ge(h_rw, a + 1)
                    dve.tensor_tensor(of[:, a, :], hb[:, 2, :], hrs[:], ALU.mult).then_inc(h_on, 1)

                def h_attended(s):
                    if s % NC == 0 and s > 0:
                        h_normalise(s // NC - 1)

                def h_attn_out():
                    dve.wait_ge(h_wo, 1)
                    dve.tensor_tensor(hres[:], hres[:], hb[:, 0:2, :], ALU.add).then_inc(h_r2, 1)

                def h_fnorm():
                    dve.wait_ge(h_rs, 3)
                    dve.wait_ge(h_r2, 1)
                    dve.tensor_tensor(hxn[:], hres[:], over_halves(hrs[:]), ALU.mult).then_inc(h_xn, 1)

                def h_up():
                    dve.wait_ge(h_si, 1)
                    for m in range(FT):
                        n = P if m < FT - 1 else FR
                        dve.wait_ge(h_u, m + 1)
                        v = gate_tile(m)[0:n]
                        dve.tensor_tensor(v, v, hb[0:n, m % 3, :], ALU.mult).then_inc(h_h, 1)

                def h_down():
                    dve.wait_ge(h_wd, 1)
                    dve.tensor_tensor(hres[:], hres[:], hb[:, 0:2, :], ALU.add).then_inc(h_r2, 1)

                steps = {"centre": h_centre, "scale": h_scale, "norm": h_norm, "qk": h_rest, "mid": h_third,
                         "max": h_max, "attend": h_attended, "last": lambda: h_normalise(NKV - 1),
                         "wo": h_attn_out, "fnorm": h_fnorm, "up": h_up, "down": h_down}
                if do_t:
                    take()
                    for l in range(NL):
                        pre(l)
                        conv(l)
                        beside(PL * l + 1, steps)
                        split(l)
                        beside(PL * l + 2, steps)
                        for g in range(G):
                            step(l, g)
                            beside(PL * l + 3 + g, steps)
                        post(l)
                    experts_norm()
                    experts_pick()
                    experts()
                else:
                    for point in range(POINTS):
                        beside(point, steps)

            def pool_program(pool):
                for l in range(NL):
                    for g in range(G):
                        k = G * l + g
                        pool.wait_ge(scanned, k + 1)
                        pool.wait_ge(c_copied, 2 * k + 2)
                        for h in range(HF):
                            v = state[k % 3][:, h, :, :]
                            pool.tensor_tensor(v, v, cs[k % 2][:], ALU.mult).then_inc(p_own, 1)
                            pool.wait_ge(p_own, HF * k + h + 1)
                            pool.tensor_tensor(v[:, 0, :], v[:, 0, :], v[:, 1, :], ALU.add
                                               ).then_inc(weighed, 1)

            with nc.Block() as block:
                block.sync(sp_program)
                block.tensor(pe_program)
                block.scalar(act_program)
                block.vector(dve_program)
                if do_t:
                    block.gpsimd(pool_program)

        turn_sems = sems[setup_sems:]

        def clear():
            for s in turn_sems:
                nc.sync.sem_clear(s)
            nc.all_engine_barrier()

        turn(0, None)
        clear()
        if B > 1:
            with nc.Fori(0, B - 1) as i:
                turn(i + 1, i)
                clear()
        turn(None, B - 1)


_INS = ["L0_attn_x", "L0_attn_attn_norm_w", "L0_attn_ffn_norm_w", "L0_attn_Wq", "L0_attn_Wk", "L0_attn_Wv",
        "L0_attn_Wo", "L0_attn_Wg", "L0_attn_Wu", "L0_attn_Wd", "L0_attn_m_norm_w", "L0_attn_Win",
        "L0_attn_conv_w", "L0_attn_conv_b", "L0_attn_Wx", "L0_attn_A_log", "L0_attn_Dp", "L0_attn_Wout",
        "L0_ffn_Wg", "L0_ffn_ln_scale", "L0_ffn_ln_bias", "L0_ffn_W1", "L0_ffn_b1", "L0_ffn_W2", "L0_ffn_b2"]


def kernel(**inputs):
    import numpy as _np
    import concourse.bacc as _bacc
    from concourse import mybir as _mybir
    from concourse.bass_utils import run_bass_kernel_spmd as _run

    nc = _bacc.Bacc("TRN2", target_bir_lowering=False, num_devices=1)
    arrays, args = {}, []
    for name in _INS:
        a = _np.ascontiguousarray(inputs[name])
        arrays[f"in_{name}_dram"] = a
        args.append(nc.dram_tensor(f"in_{name}_dram", a.shape, _mybir.dt.from_np(a.dtype), kind="ExternalInput").ap())
    shape = inputs["L0_attn_x"].shape
    args.append(nc.dram_tensor("out_0_dram", shape, _mybir.dt.float32, kind="ExternalOutput").ap())
    layered_block_kernel(nc, *args)
    r = _run(nc, [arrays], core_ids=[0])
    return r.results[0]["out_0_dram"]
```

```python
from contextlib import ExitStack

import concourse.bass as bass
from concourse import mybir

F32 = mybir.dt.float32
BF16 = mybir.dt.bfloat16
ALU = mybir.AluOpType
ACT = mybir.ActivationFunctionType
AX = mybir.AxisListType

P = 128
EPS_RMS = 1e-6
EPS_LN = 1e-5
MASKED = -1e30


def layered_block_kernel(nc, x, attn_norm_w, ffn_norm_w, Wq, Wk, Wv, Wo, Wg, Wu, Wd, m_norm_w, Win, conv_w,
                         conv_b, Wx, A_log, Dp, Wout, gate_W, ln_scale, ln_bias, W1, b1, W2, b2, out):
    B, T, D = x.shape
    HF = D // P
    NC = T // P
    NH, HD = 16, D // 16
    NKV = Wk.shape[2] // HD
    NL = Win.shape[0]
    NS = A_log.shape[2]
    KC = conv_w.shape[2]
    FF = Wg.shape[2]
    FT = -(-FF // P)
    FR = FF - (FT - 1) * P
    NE, _, EH = W1.shape
    ET = NE * EH // P
    G = NS // 2
    SCALE = float(HD) ** -0.5
    PRODUCTS = [(0, 0), (0, 1), (1, 0), (1, 1), (0, 2), (2, 0)]
    KR = len(PRODUCTS) * HD

    ctx = ExitStack()
    with ctx:
        def sb(name, shape, dt=F32):
            return ctx.enter_context(nc.sbuf_tensor(name, shape, dt))

        sems = []

        def sem(name):
            s = ctx.enter_context(nc.semaphore(name))
            sems.append(s)
            return s

        win = sb("win", [P, NL, HF, 2 * D])
        wxd = sb("wxd", [P, NL, HF, D + 2 * NS])
        wxbc = sb("wxbc", [P, NL, HF, 3 * 2 * NS])
        wout = sb("wout", [P, NL, HF, D])
        wq = sb("wq", [P, HF, D])
        wk = sb("wk", [P, HF, P])
        wv = sb("wv", [P, HF, NKV * HD])
        wo = sb("wo", [P, NKV // 2, D])
        wg = sb("wg", [P, HF, FF])
        wu = sb("wu", [P, HF, FF])
        wd = sb("wd", [P, FT, D])
        w1 = sb("w1", [P, HF, NE * EH])
        w2 = sb("w2", [P, ET, D])
        b2r = sb("b2r", [NE, D])
        gwt = sb("gwt", [P, HF, NE])
        anw = sb("anw", [P, HF])
        fnw = sb("fnw", [P, HF])
        mnw = sb("mnw", [P, NL, HF])
        cw = sb("cw", [P, NL, HF, KC])
        cb = sb("cb", [P, NL, HF])
        dp = sb("dp", [P, NL, HF])
        aneg = sb("aneg", [P, NL, HF, NS])
        lns = sb("lns", [P, HF, NE])
        lnb = sb("lnb", [P, HF, NE])
        b1c = sb("b1c", [P, ET])
        ident = sb("ident", [P, P])
        identb = sb("identb", [P, P], BF16)
        mean_w = sb("mean_w", [P, P])
        maskq = sb("maskq", [P, P], BF16)
        maskk = sb("maskk", [P, P], BF16)
        selbc = sb("selbc", [P, 2 * NS, P], BF16)
        sele = sb("sele", [NE, NE * EH], BF16)
        rank_w = sb("rank_w", [P, NC, NE])
        epsc = sb("epsc", [P, 3])
        res = sb("res", [P, HF, T])
        tA = sb("tA", [P, HF, T])
        tB = sb("tB", [P, HF, T])
        rs = sb("rs", [P, T])
        xbp = sb("xbp", [P, HF, KC - 1 + T])
        delta = xbp[:, :, KC - 1:KC - 1 + T]
        sz = sb("sz", [P, HF, T])
        xc = sb("xc", [P, HF, T])
        bcs = sb("bcs", [P, T], BF16)
        bcr = rs[0:4 * NS, :]
        decay = [sb(f"decay{k}", [P, HF, 2, T]) for k in range(2)]
        state = [sb(f"state{k}", [P, HF, 2, T]) for k in range(3)]
        cs = [sb(f"cs{k}", [P, 2, T]) for k in range(2)]
        hid = decay[0]
        x0t = cs[0]
        ers = xc[:, 0, :]
        lg = sb("lg", [P, NC, NE])
        lmx = sb("lmx", [P, NC, 1])
        oh = sb("oh", [P, NC, NE])
        oht = sz[0:NE, 0, :]
        ohtb = sz[:, 1, :].bitcast(BF16)[0:NE, 0:T]
        hres = sb("hres", [P, HF, T])
        hA = sb("hA", [P, HF, T])
        xio = hA[:].rearrange("p h t -> p (h t)").rearrange("p (c d) -> p c d", c=NC)
        hxn = sb("hxn", [P, HF, T])
        x0h = hxn
        hrs = sb("hrs", [P, T])
        parts = sb("parts", [P, 3, HF + 1, T], BF16)
        of = parts[:].rearrange("p a h t -> p (a h t)").bitcast(F32)[:, 0:NKV * T].rearrange(
            "p (g t) -> p g t", g=NKV)
        qst = sb("qst", [P, NH, T], BF16)
        kst = sb("kst", [P, NKV, T], BF16)
        vp = sb("vp", [P, NC, NKV, 2 * HD])
        side = sb("side", [P, 2])
        prob = sb("prob", [P, 4 * (2 * T - P)])
        rest = prob[:, 0:3 * T].rearrange("p (h t) -> p h t", t=T)
        hms = prob[:, 0:T]
        mx = sb("mx", [P, NC, NH])
        negm = parts[0:NH, 0, 0, :]
        qk_dram = nc.dram_tensor("qk_parts", [3, (HF + 1) * P, T], BF16).ap()
        x0_dram = nc.dram_tensor("x_by_feature", [B, P, HF * T], F32).ap()
        nm_dram = nc.dram_tensor("neg_max", [NH, T], BF16).ap()
        gb = prob[:, 0:FT * T].rearrange("p (m t) -> p m t", t=T)

        def prob_of(s):
            return prob[:, 4 * T:] if s % 2 else prob[:, 0:4 * T]

        def gate_tile(m):
            return gb[:, m, :]

        hb = ctx.enter_context(nc.psum_tensor("hb", [P, 3, T], F32))
        bb = ctx.enter_context(nc.psum_tensor("bb", [P, 2, T], F32))
        cbk = ctx.enter_context(nc.psum_tensor("cbk", [P, T], F32))
        yb = ctx.enter_context(nc.psum_tensor("yb", [P, 2, T], F32))

        half = lambda v: v.rearrange("(h p) -> p h", p=P)

        s_load = sem("s_load")
        e_store = sem("e_store")
        s_b1 = sem("s_b1")
        s_ae = sem("s_ae")
        s_dve0 = sem("s_dve0")
        s_pool0 = sem("s_pool0")
        loads = [
            (win[:], Win.rearrange("l (h p) n -> p l h n", p=P)),
            (wxd[:], Wx.rearrange("l (h p) n -> p l h n", p=P)),
            (wout[:], Wout.rearrange("l (h p) n -> p l h n", p=P)),
            (wq[:], Wq[0].rearrange("(h p) n -> p h n", p=P)),
            (wk[:, :, 0:P // 2], Wk[0].rearrange("(h p) n -> p h n", p=P)),
            (wk[:, :, P // 2:P], Wk[0].rearrange("(h p) n -> p h n", p=P)),
            (wv[:], Wv[0].rearrange("(h p) n -> p h n", p=P)),
            (wg[:], Wg[0].rearrange("(h p) n -> p h n", p=P)),
            (wu[:], Wu[0].rearrange("(h p) n -> p h n", p=P)),
            (wd[:, 0:FT - 1, :], Wd[0, 0:(FT - 1) * P].rearrange("(m p) n -> p m n", p=P)),
            (wd[0:FR, FT - 1, :], Wd[0, (FT - 1) * P:FF]),
            (w2[:], W2.rearrange("(m a) h n -> (a h) m n", a=P // EH)),
            (b2r[:], b2),
            (anw[:], half(attn_norm_w[0])),
            (fnw[:], half(ffn_norm_w[0])),
            (b1c[:], b1.rearrange("(m a) h -> (a h) m", a=P // EH)),
        ]
        for h in range(HF):
            rows = slice(h * P, h * P + P)
            loads += [
                (w1[:, h, :].rearrange("p (e n) -> p e n", e=NE), W1[:, rows, :].rearrange("e p n -> p e n")),
                (gwt[:, h, :], gate_W[:, rows].rearrange("e p -> p e")),
                (lns[:, h, :], ln_scale[:, rows].rearrange("e p -> p e")),
                (lnb[:, h, :], ln_bias[:, rows].rearrange("e p -> p e")),
                (mnw[:, :, h], m_norm_w[:, rows].rearrange("l p -> p l")),
                (cw[:, :, h, :], conv_w[:, rows, :].rearrange("l p k -> p l k")),
                (cb[:, :, h], conv_b[:, rows].rearrange("l p -> p l")),
                (dp[:, :, h], Dp[:, rows].rearrange("l p -> p l")),
                (aneg[:, :, h, :], A_log[:, rows, :].rearrange("l p n -> p l n")),
            ]

        for j in range(4):
            for e in range(2):
                row = 32 * j + e * HD
                loads.append((wo[row:row + HD], Wo[0].rearrange("(b e j i) n -> e j i b n", e=2, j=4, i=HD)[e, j]))

        with nc.Block() as block:
            @block.sync
            def _(sp):
                for dst, src in loads:
                    with nc.allow_non_contiguous_dma(reason="small columns, once"):
                        sp.dma_start(dst, src).then_inc(s_load, 16)

            @block.gpsimd
            def _(pool):
                count = [0]

                def link(ins):
                    count[0] += 1
                    ins.then_inc(s_pool0, 1)
                    pool.wait_ge(s_pool0, count[0])

                def select(t, fill, cond, base, pattern, row):
                    link(pool.affine_select(out=t, in_=t, compare_op=cond, fill=fill, base=base,
                                            pattern=pattern, channel_multiplier=row))

                for t in (ident, identb, maskq, maskk, selbc, sele):
                    link(pool.memset(t[:], 0.0))
                select(ident[:], 1.0, ALU.not_equal, 0, [[-1, P]], 1)
                select(identb[:], 1.0, ALU.not_equal, 0, [[-1, P]], 1)
                select(maskq[:], MASKED, ALU.is_ge, 0, [[-1, P]], 1)
                select(maskk[:], MASKED, ALU.is_ge, 0, [[1, P]], -1)
                for part in range(3):
                    select(selbc[:], 1.0, ALU.not_equal, -2 * NS * part, [[-1, 2 * NS], [0, P]], 1)
                select(sele[:].rearrange("e (a n) -> e a n", a=NE), 1.0, ALU.not_equal, 0,
                       [[-1, NE], [0, EH]], 1)
                link(pool.memset(mean_w[:], 1.0 / D))

            @block.scalar
            def _(act):
                act.wait_ge(s_load, 16 * len(loads))
                act.activation(aneg[:], aneg[:], ACT.Exp).then_inc(s_ae, 1)

            @block.tensor
            def _(pe):
                pe.wait_ge(s_load, 16 * len(loads))
                for m in range(ET):
                    for h in range(HF):
                        last = pe.matmul(cbk[:, m * NE:(m + 1) * NE], w1[:, h, m * P:(m + 1) * P],
                                         lnb[:, h, :], start=(h == 0), stop=(h == HF - 1))
                last.then_inc(s_b1, 1)

            @block.vector
            def _(dve):
                count = [0]

                def link(ins):
                    count[0] += 1
                    ins.then_inc(s_dve0, 1)
                    dve.wait_ge(s_dve0, count[0])

                for k in range(3):
                    dve.memset(epsc[:, k:k + 1], (EPS_RMS, EPS_LN, 1.0)[k])
                for e in range(NE):
                    dve.memset(rank_w[:, :, e], float(NE - e))
                for k in range(2):
                    dve.memset(decay[k][:, :, :, 0:1], 0.0)
                dve.memset(xbp[:, :, 0:KC - 1], 0.0)
                dve.memset(vp[:], 1.0)
                dve.memset(bcs[:], 0.0).then_inc(e_store, 16)
                dve.memset(qst[KR:P].bitcast(F32), 0.0)
                link(dve.memset(kst[KR:P].bitcast(F32), 0.0))
                dve.memset(kst[KR:KR + 1, :, :], 1.0)
                dve.wait_ge(s_pool0, 8)
                for e in range(2):
                    dve.tensor_reduce(side[:, e:e + 1], ident[:].rearrange("p (j e i) -> p e j i", e=2, i=HD)[:, e],
                                      AX.XY, ALU.add)
                dve.wait_ge(s_load, 16 * len(loads))
                for h in range(HF):
                    for w, c in ((wq, anw), (wk, anw), (wv, anw), (wg, fnw), (wu, fnw)):
                        link(dve.tensor_scalar(w[:, h, :], w[:, h, :], c[:, h:h + 1], None, ALU.mult))
                    for l in range(NL):
                        link(dve.tensor_scalar(win[:, l, h, :], win[:, l, h, :], mnw[:, l, h:h + 1], None,
                                               ALU.mult))
                for k in range(3):
                    dve.tensor_copy(wxbc[:, :, :, k * 2 * NS:(k + 1) * 2 * NS], wxd[:, :, :, D:D + 2 * NS])
                dve.wait_ge(s_ae, 1)
                dve.tensor_scalar(aneg[:], aneg[:], -1.0, None, ALU.mult)
                dve.wait_ge(s_b1, 1)
                for m in range(ET):
                    for a in range(P // EH):
                        rows = slice(a * EH, (a + 1) * EH)
                        e = m * (P // EH) + a
                        dve.tensor_tensor(b1c[rows, m:m + 1], b1c[rows, m:m + 1],
                                          cbk[rows, m * NE + e:m * NE + e + 1], ALU.add)
                for h in range(HF):
                    for e in range(NE):
                        dve.tensor_scalar(w1[:, h, e * EH:(e + 1) * EH], w1[:, h, e * EH:(e + 1) * EH],
                                          lns[:, h, e:e + 1], None, ALU.mult)


        setup_sems = len(sems)
        t_own = sem("t_own")
        t_res = sem("t_res")
        t_sq = sem("t_sq")
        t_stat = sem("t_stat")
        t_ln = sem("t_ln")
        t_rs = sem("t_rs")
        t_cen = sem("t_cen")
        t_xn = sem("t_xn")
        t_xb = sem("t_xb")
        t_z = sem("t_z")
        t_xbp = sem("t_xbp")
        t_zc = sem("t_zc")
        t_zs = sem("t_zs")
        t_conv = sem("t_conv")
        t_xc = sem("t_xc")
        t_bc = sem("t_bc")
        t_dl = sem("t_dl")
        t_split = sem("t_split")
        t_vr = sem("t_vr")
        t_abs = sem("t_abs")
        t_delta = sem("t_delta")
        t_u = sem("t_u")
        b_ready = sem("b_ready")
        b_used = sem("b_used")
        c_ready = sem("c_ready")
        c_copied = sem("c_copied")
        decay_ready = sem("decay_ready")
        scanned = sem("scanned")
        p_own = sem("p_own")
        weighed = [sem("weighed0"), sem("weighed1")]
        weighed_last = sem("weighed_last")
        summed = sem("summed")
        t_yg = sem("t_yg")
        t_out = sem("t_out")
        e_x0 = sem("e_x0")
        e_lg = sem("e_lg")
        e_oh = sem("e_oh")
        e_oht = sem("e_oht")
        e_ohc = sem("e_ohc")
        e_hp = sem("e_hp")
        e_mask = sem("e_mask")
        e_gelu = sem("e_gelu")
        e_hm = sem("e_hm")
        e_w2 = sem("e_w2")
        e_fin = sem("e_fin")
        e_ft = sem("e_ft")
        e_fc = sem("e_fc")

        h_x = sem("h_x")
        h_tr = sem("h_tr")
        h_x0 = sem("h_x0")
        h_cen = sem("h_cen")
        h_x0w = sem("h_x0w")
        h_sq = sem("h_sq")
        h_stat = sem("h_stat")
        h_vr = sem("h_vr")
        h_ln = sem("h_ln")
        h_rs = sem("h_rs")
        h_xn = sem("h_xn")
        h_q = sem("h_q")
        h_hi = sem("h_hi")
        h_lo1 = sem("h_lo1")
        h_mid = sem("h_mid")
        h_lo2 = sem("h_lo2")
        h_qkw = sem("h_qkw")
        h_qks = sem("h_qks")
        h_v = sem("h_v")
        h_vp = sem("h_vp")
        h_s = sem("h_s")
        h_mx = sem("h_mx")
        h_mt = sem("h_mt")
        h_nm = sem("h_nm")
        h_nmw = sem("h_nmw")
        h_nms = sem("h_nms")
        h_st = sem("h_st")
        h_p = sem("h_p")
        h_pv = sem("h_pv")
        h_dl = sem("h_dl")
        h_ri = sem("h_ri")
        h_ot = sem("h_ot")
        h_rw = sem("h_rw")
        h_on = sem("h_on")
        h_wo = sem("h_wo")
        h_r2 = sem("h_r2")
        h_g = sem("h_g")
        h_gc = sem("h_gc")
        h_si = sem("h_si")
        h_u = sem("h_u")
        h_h = sem("h_h")
        h_wd = sem("h_wd")

        MAXB = [[(0, 0), (P, 2)], [(0, 3)], [(0, 1)]]
        EXPB = [[[0], [1], [2], [3]], [[0], [1], [2], [3]], [[0, 1], [2, 3]], [[0, 1, 2, 3]]]
        EXPN = [len(b) for b in EXPB]
        NB = 3

        def exp_unit(s):
            return sum(EXPN) * (s // NC) + sum(EXPN[0:s % NC])

        PL = 2 * G + 4
        POINTS = NL * PL + 10
        ATTEND = [(s, part) for s in range(NH) for part in range(2 if s % NC < 2 else 1)]
        HEAD = ([("load",), ("centre",), ("var",), ("scale",), ("norm",)]
                + [("q", j) for j in range(3)] + [("qk",), ("mid",), ("v",)]
                + [("max", h) for h in range(NH)] + [("maxrow",)]
                + [("attend", s, part) for s, part in ATTEND] + [("last",)]
                + [("wo", j) for j in range(HF)] + [("fms",), ("fnorm",)]
                + [("gate", m) for m in range(FT)] + [("silu",)] + [("up", m) for m in range(FT)]
                + [("down", m) for m in range(FT)])
        PLACE = [0, 1, 2, 3, 5, 6, 7, 8, 9, 10, 11, 15, 16, 16, 17, 18, 21, 22, 22, 22, 24, 24, 24, 24,
                 24, 24, 24, 24, 26, 28, 29, 30, 30, 31, 32, 32, 34, 35, 36, 38, 39, 39, 41, 44, 45, 45, 45, 47,
                 50, 51, 52, 53, 53, 55, 55, 57, 58, 58, 59, 59, 60, 62, 62, 63, 64, 64, 65, 68, 68, 68, 69, 69,
                 69, 69, 69, 69]
        assert len(PLACE) == len(HEAD) and list(PLACE) == sorted(PLACE)
        BESIDE = [[w for w, p in zip(HEAD, PLACE) if p == point] for point in range(POINTS)]

        def scans(k):
            return k + 1 + k // G + 1

        def turn(head, tail):
            do_h, do_t = head is not None, tail is not None

            def beside(point, steps):
                if do_h:
                    for name, *which in BESIDE[point]:
                        if name in steps:
                            steps[name](*which)

            def sp_program(sp):
                if do_h:
                    sp.dma_start(xio, x[bass.ds(head, 1)].rearrange("b (c p) d -> p (b c) d", p=P)
                                 ).then_inc(h_x, 16)
                    sp.wait_ge(h_x0, 1)
                    sp.dma_start(x0_dram[bass.ds(head, 1)].rearrange("b p t -> (b p) t"),
                                 x0h[:].rearrange("p h t -> p (h t)")).then_inc(h_x0w, 16)
                    sp.wait_ge(h_x0w, 16)
                    sp.wait_ge(h_lo2, 1)
                    sp.dma_start(qk_dram.rearrange("a (h p) t -> p a h t", p=P), parts[:]).then_inc(h_qkw, 16)
                    sp.wait_ge(h_qkw, 16)
                    for n, (kpart, qpart) in enumerate(PRODUCTS):
                        rows = slice(n * HD, (n + 1) * HD)
                        sp.dma_start(qst[rows], qk_dram[qpart, 0:D].rearrange("(h j) t -> j h t", j=HD)
                                     ).then_inc(h_qks, 16)
                        sp.dma_start(kst[rows], qk_dram[kpart, D:D + NKV * HD].rearrange(
                            "(h j) t -> j h t", j=HD)).then_inc(h_qks, 16)
                    sp.wait_ge(h_nm, 1)
                    sp.dma_start(nm_dram, negm).then_inc(h_nmw, 16)
                    sp.wait_ge(h_nmw, 16)
                    sp.dma_start(qst[KR:KR + 1].rearrange("o h t -> o (h t)"),
                                 nm_dram.rearrange("(o h) t -> o (h t)", o=1)).then_inc(h_nms, 16)
                if do_t:
                    sp.wait_ge(weighed[0], G * NL)
                    sp.wait_ge(weighed[1], (G - 1) * NL)
                    sp.wait_ge(weighed_last, NL)
                    sp.dma_start(x0t[:].rearrange("p h t -> p (h t)"),
                                 x0_dram[bass.ds(tail, 1)].rearrange("b p t -> (b p) t")).then_inc(e_x0, 16)
                    sp.wait_ge(e_fc, 2)
                    sp.sem_clear(e_store)
                    sp.dma_start(out[bass.ds(tail, 1)].rearrange("b (c p) d -> p (b c) d", p=P),
                                 state[0][:].rearrange("p h n t -> p (h n t)")[:, 0:NC * D]
                                 .rearrange("p (c d) -> p c d", c=NC)).then_inc(e_store, 16)

            def pe_program(pe):
                def project(dst, w, src, cols, n=P, stop=True):
                    for h in range(HF):
                        last = pe.matmul(dst, w[:, h, cols:cols + n], src[:, h, :], start=(h == 0),
                                         stop=(h == HF - 1))
                    return last

                def stat(dst, src):
                    for h in range(HF):
                        last = pe.matmul(dst, mean_w[:], src[:, h, :], start=(h == 0), stop=(h == HF - 1))
                    return last

                def both(w, src, ready, l, done):
                    for h in range(HF):
                        pe.wait_ge(ready, HF * l + h + 1)
                        for j in range(HF):
                            last = pe.matmul(bb[:, j, :], w[:, h, j * P:(j + 1) * P], src[:, h, :],
                                             start=(h == 0), stop=(h == HF - 1))
                            if h == HF - 1:
                                last.then_inc(done, 1)

                def pre(l):
                    wl = win[:, l]
                    for j in range(HF):
                        pe.wait_ge(t_res, HF * l + j + 1)
                        pe.matmul(bb[:, j, :], wl[:, 0, j * P:(j + 1) * P], res[:, 0, :], start=True, stop=False)
                        pe.wait_ge(t_sq, HF * l + j + 1)
                        last = pe.matmul(yb[:, 0, :], mean_w[:], tA[:, j, :], start=(j == 0), stop=(j == HF - 1))
                    last.then_inc(t_stat, 1)
                    for j in range(HF):
                        pe.matmul(bb[:, j, :], wl[:, 1, j * P:(j + 1) * P], res[:, 1, :], start=False, stop=True
                                  ).then_inc(t_xb, 1)
                    beside(PL * l, steps)
                    project(cbk[:], wl, res, 2 * P).then_inc(t_z, 1)
                    project(yb[:, 1, :], wl, res, 3 * P).then_inc(t_z, 1)

                def pre_x(l):
                    for h in range(HF):
                        pe.wait_ge(t_xc, HF * l + h + 1)
                        for j in range(HF):
                            last = pe.matmul(bb[:, j, :], wxd[:, l, h, j * P:(j + 1) * P], xc[:, h, :],
                                             start=(h == 0), stop=(h == HF - 1))
                            if h == HF - 1:
                                last.then_inc(t_dl, 1)
                        if h == 0:
                            pe.wait_ge(t_zc, HF * l + 1)
                        last = pe.matmul(cbk[0:3 * 2 * NS, :], wxbc[:, l, h, :], xc[:, h, :], start=(h == 0),
                                         stop=(h == HF - 1))
                    last.then_inc(t_bc, 1)

                def spread_b(l, g):
                    k = G * l + g
                    if g == 0:
                        pe.wait_ge(t_split, l + 1)
                        pe.wait_ge(t_delta, HF * (l + 1))
                    for j in range(2):
                        if g > 0:
                            pe.wait_ge(b_used, 2 * (k - 1) + j + 1)
                        pe.matmul(bb[:, j, :], selbc[:, 2 * g + j, :], bcs[:], start=True, stop=True
                                  ).then_inc(b_ready, 1)

                def spread_c(l, g, j):
                    n = 2 * g + j
                    if n > 0:
                        pe.wait_ge(c_copied, 2 * G * l + n)
                    pe.matmul(cbk[:], selbc[:, NS + n, :], bcs[:], start=True, stop=True).then_inc(c_ready, 1)

                def sum_states(l, g):
                    k = G * l + g
                    pe.wait_ge(weighed[0], k + 1)
                    pe.matmul(yb[:, 0, :], ident[:], state[k % 3][:, 0, 0, :], start=(g == 0), stop=(g == G - 1))
                    if g < G - 1:
                        pe.wait_ge(weighed[1], (G - 1) * l + g + 1)
                    else:
                        pe.wait_ge(weighed_last, l + 1)
                    for j in range(2):
                        last = pe.matmul(yb[:, 1, :], ident[:], state[k % 3][:, 1, j, :],
                                         start=(g == 0 and j == 0), stop=(g == G - 1 and j == 1))
                    last.then_inc(summed, 1)

                def post(l):
                    both(wout[:, l], tA, t_yg, l, t_out)

                def experts_norm():
                    pe.wait_ge(t_res, HF * (NL + 1) + 1)
                    stat(yb[:, 0, :], x0t).then_inc(t_stat, 1)
                    beside(PL * NL, steps)
                    pe.wait_ge(t_sq, HF * NL + 1)
                    stat(yb[:, 1, :], tA).then_inc(t_stat, 1)
                    pe.wait_ge(t_cen, 1)
                    for c in range(NC):
                        for h in range(HF):
                            last = pe.matmul(cbk[:, c * NE:(c + 1) * NE], tB[:, h, c * P:(c + 1) * P],
                                             gwt[:, h, :], start=(h == 0), stop=(h == HF - 1))
                    last.then_inc(e_lg, 1)
                    beside(PL * NL + 1, steps)

                def experts():
                    beside(PL * NL + 2, steps)
                    pe.wait_ge(e_oh, 1)
                    for c in range(NC):
                        last = pe.transpose(cbk[0:NE, c * P:(c + 1) * P], oh[:, c, :], ident[:])
                    last.then_inc(e_oht, 1)
                    beside(PL * NL + 3, steps)
                    pe.wait_ge(t_xn, 2)
                    for m in range(ET):
                        if m >= 2:
                            pe.wait_ge(e_gelu, m - 1)
                        project(bb[:, m % 2, :], w1, tB, m * P).then_inc(e_hp, 1)
                        if m == 0:
                            pe.wait_ge(e_ohc, 1)
                        if m >= 2:
                            pe.wait_ge(e_hm, m - 1)
                        pe.matmul(yb[:, m % 2, :], sele[:, m * P:(m + 1) * P], ohtb, start=True,
                                  stop=True).then_inc(e_mask, 1)
                        beside(PL * NL + 4 + m, steps)
                    beside(PL * NL + 8, steps)
                    pe.wait_ge(e_hm, ET)
                    for j in range(2):
                        for m in range(ET):
                            pe.matmul(bb[:, j, :], w2[:, m, j * P:(j + 1) * P],
                                      hid[:, m // 2, m % 2, :], start=(m == 0), stop=False)
                        last = pe.matmul(bb[:, j, :], b2r[:, j * P:(j + 1) * P], oht, start=False, stop=True)
                    last.then_inc(e_w2, 1)
                    beside(PL * NL + 9, steps)
                    pe.wait_ge(e_fin, 1)
                    for b in range(2):
                        for c in range(2):
                            for h in range(HF):
                                last = pe.transpose(yb[:, b, c * D + h * P:c * D + h * P + P],
                                                    tA[:, h, (2 * b + c) * P:(2 * b + c + 1) * P], ident[:])
                        last.then_inc(e_ft, 1)

                def h_load():
                    pe.wait_ge(h_x, 16)
                    for h in range(HF):
                        for c in range(NC):
                            last = pe.transpose(hb[:, h, c * P:(c + 1) * P], xio[:, c, h * P:(h + 1) * P],
                                                ident[:])
                    last.then_inc(h_tr, 1)

                def h_mean():
                    pe.wait_ge(h_x0, 1)
                    stat(hb[:, 2, :], x0h).then_inc(h_stat, 1)

                def h_norm(m, bank):
                    pe.wait_ge(h_sq, m)
                    stat(hb[:, bank, :], hxn).then_inc(h_stat, 1)

                def h_qk(j):
                    pe.wait_ge(h_xn, 1)
                    if j < HF:
                        project(hb[:, j, :], wq, hxn, j * P)
                    else:
                        project(hb[:, 2, :], wk, hxn, 0).then_inc(h_q, 1)

                def h_values():
                    pe.wait_ge(h_lo2, 1)
                    for c in range(NC):
                        for h in range(HF):
                            last = pe.matmul(hb[:, 0, c * 64:(c + 1) * 64], hxn[:, h, c * P:(c + 1) * P],
                                             wv[:, h, :], start=(h == 0), stop=(h == HF - 1))
                    last.then_inc(h_v, 1)

                def h_max(h):
                    if h == 0:
                        pe.wait_ge(h_vp, 1)
                        pe.wait_ge(h_qks, 32 * len(PRODUCTS))
                    for b in range(NB):
                        if h > 0:
                            pe.wait_ge(h_mx, NB * (h - 1) + b + 1)
                        for col, c in MAXB[b]:
                            n = (c + 1) * P
                            pe.matmul(hb[:, b, col:col + n], qst[0:KR, h, c * P:n], kst[0:KR, h // 4, 0:n],
                                      start=True, stop=False)
                            last = pe.matmul(hb[:, b, col + n - P:col + n], identb[:], maskq[:],
                                             start=False, stop=True)
                        last.then_inc(h_s, 1)

                def h_maxrow():
                    pe.wait_ge(h_mx, NB * NH)
                    for c in range(NC):
                        last = pe.transpose(hb[0:NH, 0, c * P:(c + 1) * P], mx[:, c, :], ident[:])
                    last.then_inc(h_mt, 1)

                def h_attend(s, part):
                    a, c = divmod(s, NC)
                    n = T - c * P
                    if s == 0:
                        pe.wait_ge(h_nms, 16)
                    for b, heads in list(enumerate(EXPB[c]))[2 * part:2 * part + 2]:
                        w = exp_unit(s) + b
                        if w >= 2:
                            pe.wait_ge(h_p, w - 1)
                        for i, j in enumerate(heads):
                            pe.matmul(hb[:, w % 2, i * n:(i + 1) * n], kst[:, a, c * P:(c + 1) * P],
                                      qst[:, 4 * a + j, c * P:T], start=True, stop=False)
                            last = pe.matmul(hb[:, w % 2, i * n:i * n + P], identb[:], maskk[:], start=False,
                                             stop=True)
                        last.then_inc(h_st, 1)
                    if part == 0 and s > 0:
                        h_weigh(s - 1)

                def h_weigh(s):
                    a, c = divmod(s, NC)
                    n = T - c * P
                    pe.wait_ge(h_p, exp_unit(s + 1))
                    if c == 0 and a > 0:
                        pe.wait_ge(h_ot, a)
                    v = prob_of(s)
                    for j in range(4):
                        last = pe.matmul(hb[32 * j:32 * j + 32, 2, c * P:T], vp[:, c, a, :],
                                         v[:, j * n:(j + 1) * n], start=(c == 0), stop=(c == NC - 1))
                    last.then_inc(h_pv, 1)

                def h_attn_out(j):
                    pe.wait_ge(h_on, NKV)
                    for a in range(0, NKV, 2):
                        last = pe.matmul(hb[:, j, :], wo[:, a // 2, j * P:(j + 1) * P], of[:, a, :],
                                         start=(a == 0), stop=(a == NKV - 2))
                    last.then_inc(h_wo, 1)

                def h_ffn_gate(m):
                    n = P if m < FT - 1 else FR
                    if m == 0:
                        pe.wait_ge(h_xn, 2)
                    if m >= 3:
                        pe.wait_ge(h_gc, m - 2)
                    project(hb[0:n, m % 3, :], wg, hxn, m * P, n).then_inc(h_g, 1)

                def h_ffn_up(m):
                    n = P if m < FT - 1 else FR
                    pe.wait_ge(h_gc, FT - 2 + m if m < 3 else FT)
                    if m >= 3:
                        pe.wait_ge(h_h, m - 2)
                    project(hb[0:n, m % 3, :], wu, hxn, m * P, n).then_inc(h_u, 1)

                def h_ffn_down(m):
                    n = P if m < FT - 1 else FR
                    if m == 0:
                        pe.wait_ge(h_h, FT)
                    for j in range(HF):
                        last = pe.matmul(hb[:, j, :], wd[0:n, m, j * P:(j + 1) * P], gate_tile(m)[0:n],
                                         start=(m == 0), stop=(m == FT - 1))
                    if m == FT - 1:
                        last.then_inc(h_wd, 1)

                steps = {"load": h_load, "centre": h_mean, "var": lambda: h_norm(1, 0),
                         "q": h_qk, "v": h_values, "max": h_max, "maxrow": h_maxrow, "attend": h_attend,
                         "last": lambda: h_weigh(NH - 1), "wo": h_attn_out, "fms": lambda: h_norm(2, 2),
                         "gate": h_ffn_gate, "up": h_ffn_up, "down": h_ffn_down}
                if do_t:
                    for l in range(NL):
                        pre(l)
                        beside(PL * l + 1, steps)
                        pre_x(l)
                        beside(PL * l + 2, steps)
                        spread_b(l, 0)
                        for j in range(2):
                            spread_c(l, 0, j)
                        for g in range(G):
                            if g < G - 1:
                                spread_b(l, g + 1)
                                spread_c(l, g + 1, 0)
                            beside(PL * l + 3 + 2 * g, steps)
                            if g > 0:
                                sum_states(l, g - 1)
                            if g < G - 1:
                                spread_c(l, g + 1, 1)
                            beside(PL * l + 4 + 2 * g, steps)
                        sum_states(l, G - 1)
                        beside(PL * l + 3 + 2 * G, steps)
                        post(l)
                    experts_norm()
                    experts()
                else:
                    for point in range(POINTS):
                        beside(point, steps)

            def act_program(act):
                def exp_and_log():
                    act.preload_act_table_set("natural_log_exp_and_others")

                def root(dst, src, eps, ln, rs_sem, n):
                    act.activation(dst, src, ACT.Ln, bias=epsc[:, eps:eps + 1]).then_inc(ln, 1)
                    act.wait_ge(ln, n)
                    act.activation(dst, dst, ACT.Exp, scale=-0.5).then_inc(rs_sem, 1)

                def pre(l):
                    for h in range(HF):
                        act.wait_ge(t_res, HF * l + h + 1)
                        act.activation(tA[:, h, :], res[:, h, :], ACT.Square).then_inc(t_sq, 1)
                    act.wait_ge(t_stat, l + 1)
                    root(rs[:], yb[:, 0, :], 0, t_ln, t_rs, l + 1)
                    beside(PL * l, steps)
                    act.preload_act_table_set("silu_and_others")
                    for h, z in enumerate((cbk[:], yb[:, 1, :])):
                        act.wait_ge(t_z, HF * l + h + 1)
                        act.activation(sz[:, h, :], z, ACT.Copy).then_inc(t_zc, 1)
                        act.wait_ge(t_conv, HF * l + h + 1)
                        act.activation(xc[:, h, :], tA[:, h, :], ACT.Silu).then_inc(t_xc, 1)
                    act.wait_ge(t_zs, HF * (l + 1))
                    act.activation(sz[:], sz[:], ACT.Silu)
                    exp_and_log()

                def softplus(l):
                    for h in range(HF):
                        act.wait_ge(t_dl, HF * l + h + 1)
                        act.activation(tA[:, h, :], bb[:, h, :], ACT.Abs).then_inc(t_abs, 1)
                    for h in range(HF):
                        act.wait_ge(t_abs, 3 * HF * l + h + 1)
                        act.activation(tA[:, h, :], tA[:, h, :], ACT.Exp, scale=-1.0).then_inc(t_abs, 1)
                    for h in range(HF):
                        act.wait_ge(t_abs, 3 * HF * l + HF + h + 1)
                        act.activation(tA[:, h, :], tA[:, h, :], ACT.Ln, bias=epsc[:, 2:3]).then_inc(t_abs, 1)

                def decays(l, g, h):
                    k = G * l + g
                    if g == 0:
                        act.wait_ge(t_delta, HF * l + h + 1)
                    elif k >= 2:
                        act.wait_ge(scanned, scans(k - 2))
                    for j in range(2):
                        last = act.activation(decay[k % 2][:, h, j, 1:T], delta[:, h, 1:T], ACT.Exp,
                                              scale=aneg[:, l, h, 2 * g + j:2 * g + j + 1])
                    last.then_inc(decay_ready, 1)

                def copy_c(l, g, j):
                    k = G * l + g
                    if g >= 2:
                        act.wait_ge(weighed[0], k - 1)
                        act.wait_ge(weighed[1], (G - 1) * l + g - 1)
                    act.wait_ge(c_ready, 2 * k + j + 1)
                    act.activation(cs[k % 2][:, j, :], cbk[:], ACT.Copy).then_inc(c_copied, 1)

                def experts_norm():
                    beside(PL * NL, steps)
                    act.wait_ge(t_cen, 1)
                    act.activation(tA[:], tB[:], ACT.Square).then_inc(t_sq, 1)
                    act.wait_ge(t_stat, NL + 2)
                    root(rs[:], yb[:, 1, :], 1, t_ln, t_rs, NL + 1)
                    beside(PL * NL + 1, steps)
                    act.wait_ge(t_vr, 2)
                    root(ers, ers, 1, t_ln, t_rs, NL + 2)

                def experts():
                    beside(PL * NL + 2, steps)
                    act.wait_ge(e_oht, 1)
                    act.activation(oht, cbk[0:NE, :], ACT.Copy)
                    act.activation(ohtb, cbk[0:NE, :], ACT.Copy).then_inc(e_ohc, 1)
                    beside(PL * NL + 3, steps)
                    for m in range(ET):
                        act.wait_ge(e_hp, m + 1)
                        act.activation(hid[:, m // 2, m % 2, :], bb[:, m % 2, :], ACT.Gelu,
                                       bias=b1c[:, m:m + 1]).then_inc(e_gelu, 1)
                        beside(PL * NL + 4 + m, steps)
                    exp_and_log()
                    beside(PL * NL + 8, steps)
                    beside(PL * NL + 9, steps)
                    fin = state[0][:].rearrange("p h n t -> p (h n t)")
                    for b in range(2):
                        act.wait_ge(e_ft, b + 1)
                        act.activation(fin[:, b * 2 * D:(b + 1) * 2 * D], yb[:, b, :], ACT.Copy
                                       ).then_inc(e_fc, 1)

                def h_load():
                    act.wait_ge(h_tr, 1)
                    act.activation(x0h[:], hb[:, 0:2, :], ACT.Copy).then_inc(h_x0, 1)

                def h_square(src):
                    act.wait_ge(h_x0w, 16)
                    act.activation(hxn[:], src, ACT.Square).then_inc(h_sq, 1)

                def h_root(m, bank, eps):
                    act.wait_ge(h_stat, m + 1)
                    root(hrs[:], hb[:, bank, :], eps, h_ln, h_rs, m if m == 1 else 3)

                def h_root_ms():
                    act.wait_ge(h_vr, 2)
                    root(hms[:], hms[:], 0, h_ln, h_rs, 2)

                def h_var():
                    act.wait_ge(h_cen, 1)
                    h_square(hA[:])

                def h_first():
                    act.wait_ge(h_q, 1)
                    act.activation(parts[:, 0], hb[:], ACT.Copy).then_inc(h_hi, 1)

                def h_mid_():
                    act.wait_ge(h_lo1, 1)
                    act.activation(parts[:, 1], rest, ACT.Copy).then_inc(h_mid, 1)

                def h_values():
                    act.wait_ge(h_v, 1)
                    for e in range(2):
                        last = act.activation(vp[:, :, e::2, e * HD:(e + 1) * HD], hb[:, 0, 0:NC * 64].rearrange(
                            "p (c g j) -> p c g j", c=NC, g=NKV)[:, :, e::2, :], ACT.Copy)
                    last.then_inc(h_vp, 1)

                def h_negmax():
                    act.wait_ge(h_mt, 1)
                    act.activation(negm, hb[0:NH, 0, :], ACT.Copy, scale=-1.0).then_inc(h_nm, 1)

                def h_probs(s, part):
                    c = s % NC
                    n = T - c * P
                    if part == 0 and s >= 2:
                        act.wait_ge(h_pv, s - 1)
                    v = prob_of(s)
                    for b, heads in list(enumerate(EXPB[c]))[2 * part:2 * part + 2]:
                        w = exp_unit(s) + b
                        act.wait_ge(h_st, w + 1)
                        act.activation(v[:, heads[0] * n:(heads[-1] + 1) * n], hb[:, w % 2, 0:len(heads) * n],
                                       ACT.Exp, scale=SCALE).then_inc(h_p, 1)
                    if c == 0 and part == 1 and s > 0:
                        h_take(s // NC - 1)
                    if c == 2 and s > NC:
                        h_inv(s // NC - 1)

                def h_take(a):
                    act.wait_ge(h_pv, NC * (a + 1))
                    act.activation(of[:, a, :], hb[:, 2, :], ACT.Copy).then_inc(h_ot, 1)

                def h_inv(a):
                    act.wait_ge(h_rw, a + 1)
                    act.activation(hrs[:], hrs[:], ACT.Ln).then_inc(h_dl, 1)
                    act.wait_ge(h_dl, a + 1)
                    act.activation(hrs[:], hrs[:], ACT.Exp, scale=-1.0).then_inc(h_ri, 1)

                def h_last():
                    h_take(NKV - 1)
                    h_inv(NKV - 1)

                def h_fms():
                    act.wait_ge(h_r2, HF)
                    h_square(hres[:])

                def h_gate(m):
                    n = P if m < FT - 1 else FR
                    act.wait_ge(h_g, m + 1)
                    act.activation(gate_tile(m)[0:n], hb[0:n, m % 3, :], ACT.Copy).then_inc(h_gc, 1)

                def h_silu():
                    act.wait_ge(h_gc, FT)
                    act.activation(gb[:, 0:FT - 1], gb[:, 0:FT - 1], ACT.Silu)
                    act.activation(gb[0:FR, FT - 1], gb[0:FR, FT - 1], ACT.Silu).then_inc(h_si, 1)
                    exp_and_log()

                steps = {"load": h_load, "var": h_var, "scale": lambda: h_root(1, 0, 1),
                         "norm": h_root_ms, "qk": h_first, "mid": h_mid_, "v": h_values,
                         "maxrow": h_negmax, "attend": h_probs, "last": h_last, "fms": h_fms,
                         "fnorm": lambda: h_root(2, 2, 0), "gate": h_gate, "silu": h_silu}
                exp_and_log()
                if do_t:
                    for l in range(NL):
                        pre(l)
                        beside(PL * l + 1, steps)
                        softplus(l)
                        beside(PL * l + 2, steps)
                        for h in range(HF):
                            decays(l, 0, h)
                            copy_c(l, 0, h)
                        for g in range(G):
                            if g < G - 1:
                                decays(l, g + 1, 0)
                            beside(PL * l + 3 + 2 * g, steps)
                            if g < G - 1:
                                copy_c(l, g + 1, 0)
                                decays(l, g + 1, 1)
                                copy_c(l, g + 1, 1)
                            beside(PL * l + 4 + 2 * g, steps)
                        beside(PL * l + 3 + 2 * G, steps)
                    experts_norm()
                    experts()
                else:
                    for point in range(POINTS):
                        beside(point, steps)

            def dve_program(dve):
                own = [0]

                def link(ins):
                    own[0] += 1
                    ins.then_inc(t_own, 1)
                    dve.wait_ge(t_own, own[0])

                def over_halves(v, n=HF):
                    return v.rearrange("p (a t) -> p a t", a=1).broadcast_to([P, n, T])

                def take():
                    for h in range(HF):
                        dve.tensor_copy(res[:, h, :], hres[:, h, :]).then_inc(t_res, 1)

                def pre(l):
                    dve.wait_ge(t_rs, l + 1)
                    for h in range(HF):
                        dve.wait_ge(t_xb, HF * l + h + 1)
                        dve.tensor_tensor(xbp[:, h, KC - 1:KC - 1 + T], bb[:, h, :], rs[:], ALU.mult
                                          ).then_inc(t_xbp, 1)
                    beside(PL * l, steps)

                def conv(l):
                    for h in range(HF):
                        dve.wait_ge(t_xbp, HF * l + h + 1)
                        last = dve.tensor_scalar(tA[:, h, :], xbp[:, h, 0:T], cw[:, l, h, 0:1],
                                                 cb[:, l, h:h + 1], ALU.mult, ALU.add)
                        for k in range(1, KC):
                            link(last)
                            last = dve.scalar_tensor_tensor(out=tA[:, h, :], in0=xbp[:, h, k:k + T],
                                                            scalar=cw[:, l, h, k:k + 1], in1=tA[:, h, :],
                                                            op0=ALU.mult, op1=ALU.add)
                        last.then_inc(t_conv, 1)

                def split(l):
                    dve.wait_ge(t_bc, l + 1)
                    dve.wait_ge(t_zs, HF * (l + 1))
                    link(dve.tensor_copy(bcs[0:6 * NS, :], cbk[0:6 * NS, :]))
                    link(dve.tensor_tensor(bcr, cbk[0:4 * NS, :], bcs[0:4 * NS, :], ALU.subtract))
                    link(dve.tensor_copy(bcs[0:4 * NS, :], bcr))
                    dve.tensor_tensor(bcs[0:2 * NS, :], bcr[0:2 * NS, :], bcs[0:2 * NS, :],
                                      ALU.subtract).then_inc(t_split, 1)
                    for h in range(HF):
                        dve.wait_ge(t_abs, 3 * HF * l + 2 * HF + h + 1)
                        dve.scalar_tensor_tensor(out=delta[:, h, :], in0=bb[:, h, :], scalar=0.0,
                                                 in1=tA[:, h, :], op0=ALU.max, op1=ALU.add
                                                 ).then_inc(t_delta, 1)
                    for h in range(HF):
                        dve.wait_ge(t_delta, HF * l + h + 1)
                        dve.tensor_tensor(tB[:, h, :], delta[:, h, :], xc[:, h, :], ALU.mult
                                          ).then_inc(t_u, 1)

                def first(l):
                    k = G * l
                    if l == 0:
                        dve.wait_ge(e_store, 16)
                    if k >= 3:
                        dve.wait_ge(summed, k - 2)
                    for h in range(HF):
                        dve.wait_ge(t_u, HF * l + h + 1)
                        for j in range(2):
                            if h == 0:
                                dve.wait_ge(b_ready, 2 * k + j + 1)
                            last = dve.tensor_tensor(state[k % 3][:, h, j, :], tB[:, h, :], bb[:, j, :],
                                                     ALU.mult)
                            if h == HF - 1:
                                last.then_inc(b_used, 1)
                        if h == 0:
                            link(last)
                        else:
                            dve.wait_ge(b_used, 2 * k + 2)
                        dve.wait_ge(decay_ready, HF * k + h + 1)
                        flat = state[k % 3][:, h].rearrange("p n t -> p (n t)")
                        dve.tensor_tensor_scan(flat, decay[k % 2][:, h].rearrange("p n t -> p (n t)"), flat,
                                               0.0, ALU.mult, ALU.add).then_inc(scanned, 1)

                def enter(l, g):
                    k = G * l + g
                    if k >= 3:
                        dve.wait_ge(summed, k - 2)
                    for j in range(2):
                        dve.wait_ge(b_ready, 2 * k + j + 1)
                        dve.tensor_tensor(state[k % 3][:, :, j, :], tB[:], over_halves(bb[:, j, :]),
                                          ALU.mult).then_inc(b_used, 1)

                def scan(l, g):
                    k = G * l + g
                    dve.wait_ge(b_used, 2 * k + 2)
                    dve.wait_ge(decay_ready, HF * (k + 1))
                    flat = state[k % 3][:].rearrange("p h n t -> p (h n t)")
                    dve.tensor_tensor_scan(flat, decay[k % 2][:].rearrange("p h n t -> p (h n t)"), flat, 0.0,
                                           ALU.mult, ALU.add).then_inc(scanned, 1)

                def weigh_last(l):
                    k = G * l + G - 1
                    dve.wait_ge(scanned, scans(k))
                    dve.wait_ge(c_copied, 2 * k + 2)
                    v = state[k % 3][:, 1]
                    dve.tensor_tensor(v, v, cs[k % 2][:], ALU.mult).then_inc(weighed_last, 1)

                def post(l):
                    dve.wait_ge(summed, G * (l + 1))
                    beside(PL * l + 3 + 2 * G, steps)
                    for h in range(HF):
                        link(dve.scalar_tensor_tensor(out=tA[:, h, :], in0=xc[:, h, :],
                                                      scalar=dp[:, l, h:h + 1], in1=yb[:, h, :],
                                                      op0=ALU.mult, op1=ALU.add))
                        dve.tensor_tensor(tA[:, h, :], tA[:, h, :], sz[:, h, :], ALU.mult).then_inc(t_yg, 1)
                    for h in range(HF):
                        dve.wait_ge(t_out, HF * l + h + 1)
                        dve.tensor_tensor(res[:, h, :], res[:, h, :], bb[:, h, :], ALU.add).then_inc(t_res, 1)

                def experts_norm():
                    dve.wait_ge(e_x0, 16)
                    dve.wait_ge(t_res, HF * (NL + 1))
                    dve.tensor_tensor(x0t[:], x0t[:], res[:], ALU.add).then_inc(t_res, 1)
                    dve.wait_ge(t_stat, NL + 1)
                    dve.wait_ge(t_res, HF * (NL + 1) + 1)
                    dve.tensor_tensor(tB[:], x0t[:], over_halves(yb[:, 0, :]), ALU.subtract
                                      ).then_inc(t_cen, 1)
                    beside(PL * NL, steps)
                    dve.wait_ge(t_cen, 1)
                    dve.wait_ge(t_rs, NL + 1)
                    dve.tensor_tensor(ers, rs[:], yb[:, 1, :], ALU.mult).then_inc(t_vr, 1)
                    dve.wait_ge(t_vr, 1)
                    dve.tensor_tensor(ers, ers, rs[:], ALU.mult).then_inc(t_vr, 1)
                    dve.wait_ge(e_lg, 1)
                    dve.tensor_tensor(tB[:], tB[:], over_halves(rs[:]), ALU.mult).then_inc(t_xn, 1)

                def experts_pick():
                    beside(PL * NL + 1, steps)
                    dve.wait_ge(e_lg, 1)
                    link(dve.tensor_copy(lg[:], cbk[:, 0:NC * NE].rearrange("p (c e) -> p c e", c=NC)))
                    link(dve.tensor_reduce(lmx[:], lg[:], AX.X, ALU.max))
                    link(dve.tensor_tensor(lg[:], lg[:], lmx[:].broadcast_to([P, NC, NE]), ALU.is_ge))
                    link(dve.tensor_tensor(lg[:], lg[:], rank_w[:], ALU.mult))
                    link(dve.tensor_reduce(lmx[:], lg[:], AX.X, ALU.max))
                    dve.tensor_tensor(oh[:], lg[:], lmx[:].broadcast_to([P, NC, NE]), ALU.is_equal
                                      ).then_inc(e_oh, 1)

                def experts():
                    beside(PL * NL + 2, steps)
                    dve.wait_ge(t_rs, NL + 2)
                    dve.wait_ge(t_xn, 1)
                    dve.tensor_tensor(tB[:], tB[:], over_halves(ers), ALU.mult).then_inc(t_xn, 1)
                    beside(PL * NL + 3, steps)
                    for m in range(ET):
                        dve.wait_ge(e_gelu, m + 1)
                        dve.wait_ge(e_mask, m + 1)
                        v = hid[:, m // 2, m % 2, :]
                        dve.tensor_tensor(v, v, yb[:, m % 2, :], ALU.mult).then_inc(e_hm, 1)
                        beside(PL * NL + 4 + m, steps)
                    beside(PL * NL + 8, steps)
                    dve.wait_ge(e_w2, 1)
                    dve.tensor_tensor(tA[:], x0t[:], bb[:], ALU.add).then_inc(e_fin, 1)
                    beside(PL * NL + 9, steps)
                    dve.memset(hid[:, :, :, 0:1], 0.0)

                def h_centre():
                    dve.wait_ge(h_stat, 1)
                    dve.tensor_tensor(hA[:], x0h[:], over_halves(hb[:, 2, :]), ALU.subtract).then_inc(h_cen, 1)

                def h_scale():
                    dve.wait_ge(h_cen, 1)
                    dve.wait_ge(h_rs, 1)
                    dve.tensor_tensor(hms[:], hrs[:], hb[:, 0, :], ALU.mult).then_inc(h_vr, 1)
                    dve.wait_ge(h_vr, 1)
                    dve.tensor_tensor(hms[:], hms[:], hrs[:], ALU.mult).then_inc(h_vr, 1)
                    dve.tensor_tensor(hres[:], hA[:], over_halves(hrs[:]), ALU.mult).then_inc(h_cen, 1)

                def h_norm():
                    dve.wait_ge(h_cen, 2)
                    dve.wait_ge(h_rs, 2)
                    dve.tensor_tensor(hxn[:], hres[:], over_halves(hms[:]), ALU.mult).then_inc(h_xn, 1)

                def h_rest():
                    dve.wait_ge(h_hi, 1)
                    dve.tensor_tensor(rest, hb[:], parts[:, 0], ALU.subtract).then_inc(h_lo1, 1)

                def h_third():
                    dve.wait_ge(h_mid, 1)
                    dve.tensor_tensor(parts[:, 2], rest, parts[:, 1], ALU.subtract).then_inc(h_lo2, 1)

                def h_max(h):
                    for b in range(NB):
                        dve.wait_ge(h_s, NB * h + b + 1)
                        for col, c in MAXB[b]:
                            last = dve.tensor_reduce(mx[:, c, h:h + 1], hb[:, b, col:col + (c + 1) * P], AX.X,
                                                     ALU.max)
                        last.then_inc(h_mx, 1)

                def h_sums(a):
                    dve.wait_ge(h_ot, a + 1)
                    if a > 0:
                        dve.wait_ge(h_on, a)
                    dve.stream_shuffle(hrs[:], of[:, a, :], [(1 - a % 2) * HD + i % HD for i in range(32)]).then_inc(h_rw, 1)

                def h_normalise(a):
                    dve.wait_ge(h_ri, a + 1)
                    last = dve.scalar_tensor_tensor(out=of[:, a, :], in0=of[:, a, :],
                                                    scalar=side[:, a % 2:a % 2 + 1], in1=hrs[:],
                                                    op0=ALU.mult, op1=ALU.mult)
                    if a % 2:
                        link(last)
                        last = dve.tensor_tensor(of[:, a - 1, :], of[:, a - 1, :], of[:, a, :], ALU.add)
                    last.then_inc(h_on, 1)

                def h_attended(s, part):
                    if part:
                        return
                    if s % NC == 1 and s > NC:
                        h_sums(s // NC - 1)
                    if s % NC == 3 and s > NC:
                        h_normalise(s // NC - 1)

                def h_last():
                    h_sums(NKV - 1)
                    h_normalise(NKV - 1)

                def h_attn_out(j):
                    dve.wait_ge(h_wo, j + 1)
                    dve.tensor_tensor(hres[:, j, :], hres[:, j, :], hb[:, j, :], ALU.add).then_inc(h_r2, 1)

                def h_fnorm():
                    dve.wait_ge(h_rs, 3)
                    dve.wait_ge(h_r2, HF)
                    dve.tensor_tensor(hxn[:], hres[:], over_halves(hrs[:]), ALU.mult).then_inc(h_xn, 1)

                def h_up(m):
                    n = P if m < FT - 1 else FR
                    dve.wait_ge(h_si, 1)
                    dve.wait_ge(h_u, m + 1)
                    v = gate_tile(m)[0:n]
                    dve.tensor_tensor(v, v, hb[0:n, m % 3, :], ALU.mult).then_inc(h_h, 1)

                def h_down(m):
                    if m == FT - 1:
                        dve.wait_ge(h_wd, 1)
                        dve.tensor_tensor(hres[:], hres[:], hb[:, 0:2, :], ALU.add).then_inc(h_r2, 1)

                steps = {"centre": h_centre, "scale": h_scale, "norm": h_norm, "qk": h_rest, "mid": h_third,
                         "max": h_max, "attend": h_attended, "last": h_last,
                         "wo": h_attn_out, "fnorm": h_fnorm, "up": h_up, "down": h_down}
                if do_t:
                    take()
                    for l in range(NL):
                        pre(l)
                        conv(l)
                        beside(PL * l + 1, steps)
                        split(l)
                        beside(PL * l + 2, steps)
                        for g in range(G):
                            if g == 0:
                                first(l)
                            else:
                                scan(l, g)
                            if g == G - 1:
                                weigh_last(l)
                            if g < G - 1:
                                enter(l, g + 1)
                            beside(PL * l + 3 + 2 * g, steps)
                            beside(PL * l + 4 + 2 * g, steps)
                        post(l)
                    experts_norm()
                    experts_pick()
                    experts()
                else:
                    for point in range(POINTS):
                        beside(point, steps)

            def pool_program(pool):
                for l in range(NL):
                    pool.wait_ge(t_rs, l + 1)
                    for h in range(HF):
                        pool.wait_ge(t_zc, HF * l + h + 1)
                        pool.tensor_tensor(sz[:, h, :], sz[:, h, :], rs[:], ALU.mult).then_inc(t_zs, 1)
                    for g in range(G):
                        k = G * l + g
                        pool.wait_ge(c_copied, 2 * k + 2)
                        pool.wait_ge(scanned, scans(k) - (1 if g == 0 else 0))
                        v = state[k % 3][:, 0]
                        pool.tensor_tensor(v, v, cs[k % 2][:], ALU.mult).then_inc(p_own, 1)
                        pool.wait_ge(p_own, k + 1)
                        pool.tensor_tensor(v[:, 0, :], v[:, 0, :], v[:, 1, :], ALU.add
                                           ).then_inc(weighed[0], 1)
                        if g < G - 1:
                            if g == 0:
                                pool.wait_ge(scanned, scans(k))
                            v = state[k % 3][:, 1]
                            pool.tensor_tensor(v, v, cs[k % 2][:], ALU.mult).then_inc(weighed[1], 1)

            with nc.Block() as block:
                block.sync(sp_program)
                block.tensor(pe_program)
                block.scalar(act_program)
                block.vector(dve_program)
                if do_t:
                    block.gpsimd(pool_program)

        turn_sems = sems[setup_sems:]

        def clear():
            engines = (nc.sync, nc.tensor, nc.scalar, nc.vector, nc.gpsimd)
            for n, s in enumerate(turn_sems):
                engines[n % len(engines)].sem_clear(s)
            nc.all_engine_barrier()

        turn(0, None)
        clear()
        if B > 1:
            with nc.Fori(0, B - 1) as i:
                turn(i + 1, i)
                clear()
        turn(None, B - 1)
        nc.sync.wait_ge(e_store, 16)


_INS = ["L0_attn_x", "L0_attn_attn_norm_w", "L0_attn_ffn_norm_w", "L0_attn_Wq", "L0_attn_Wk", "L0_attn_Wv",
        "L0_attn_Wo", "L0_attn_Wg", "L0_attn_Wu", "L0_attn_Wd", "L0_attn_m_norm_w", "L0_attn_Win",
        "L0_attn_conv_w", "L0_attn_conv_b", "L0_attn_Wx", "L0_attn_A_log", "L0_attn_Dp", "L0_attn_Wout",
        "L0_ffn_Wg", "L0_ffn_ln_scale", "L0_ffn_ln_bias", "L0_ffn_W1", "L0_ffn_b1", "L0_ffn_W2", "L0_ffn_b2"]


def kernel(**inputs):
    import numpy as _np
    import concourse.bacc as _bacc
    from concourse import mybir as _mybir
    from concourse.bass_utils import run_bass_kernel_spmd as _run

    nc = _bacc.Bacc("TRN2", target_bir_lowering=False, num_devices=1)
    arrays, args = {}, []
    for name in _INS:
        a = _np.ascontiguousarray(inputs[name])
        arrays[f"in_{name}_dram"] = a
        args.append(nc.dram_tensor(f"in_{name}_dram", a.shape, _mybir.dt.from_np(a.dtype), kind="ExternalInput").ap())
    shape = inputs["L0_attn_x"].shape
    args.append(nc.dram_tensor("out_0_dram", shape, _mybir.dt.float32, kind="ExternalOutput").ap())
    layered_block_kernel(nc, *args)
    r = _run(nc, [arrays], core_ids=[0])
    return r.results[0]["out_0_dram"]
```
